# Optimizing a Trainium2 kernel written in Bass

```python
import numpy as np
import jax
import jax.numpy as jnp

def _softmax(x, axis=-1):
    return jax.nn.softmax(x, axis=axis)

def _gelu(x):
    return jax.nn.gelu(x, approximate=True)

def _silu(x):
    return jax.nn.silu(x)

def _sigmoid(x):
    return jax.nn.sigmoid(x)

def _layernorm(x, axis=-1, eps=1e-05):
    m = jnp.mean(x, axis=axis, keepdims=True)
    v = jnp.var(x, axis=axis, keepdims=True)
    return (x - m) / jnp.sqrt(v + eps)

def _scatter_add(tgt, idx, src, axis=0):
    return tgt.at[idx].add(src)

def _segment_sum(src, seg, n):
    return jax.ops.segment_sum(src, seg, n)
kernel_name = 'mk_flamingo_gated_d1_seqx_r8_914043'

def setup_inputs(seed: int=0):
    np.random.seed(seed)
    _w = jnp.asarray

    def _rec_inputs():
        import jax
        import jax.numpy as jnp
        _rk = jax.random.key(seed)
        x = 6.313e-05 + 0.9998 * jax.random.normal(jax.random.fold_in(_rk, 1), (4, 256, 128), jnp.float32)
        _lenS = 256 - jax.random.randint(jax.random.fold_in(_rk, 7), (4,), 0, max(1, 256 // 4) + 1, jnp.int32)
        _lenS2 = 256 - jax.random.randint(jax.random.fold_in(_rk, 8), (4,), 0, max(1, 256 // 4) + 1, jnp.int32)
        _ctx_1024P = jax.random.normal(jax.random.fold_in(_rk, 11), (4, 16, 128), jnp.float32)
        _ctx_1024c = jax.random.dirichlet(jax.random.fold_in(_rk, 511), 0.3 * jnp.ones((16,), jnp.float32), (4, 256))
        _ctx_1024t = jnp.einsum('bsk,bkd->bsd', _ctx_1024c, _ctx_1024P)
        _ctx_1024t = _ctx_1024t * jax.lax.rsqrt(jnp.mean(jnp.square(_ctx_1024t)) + 1e-12) * 0.953939
        ctx_1024 = -0.000214406 + 1.00034 * (_ctx_1024t + 0.3 * jax.random.normal(jax.random.fold_in(_rk, 611), (4, 256, 128), jnp.float32))
        _g = jax.random.normal(jax.random.fold_in(_rk, 9001), (2, 1), jnp.float32)
        _g = jnp.sign(_g) * jnp.maximum(jnp.abs(_g), 1.0) + (_g == 0) * 1.0
        g_xattn = _g[0]
        g_ffn = _g[1]
        return (x, ctx_1024, g_xattn, g_ffn)
    x, ctx_1024, g_xattn, g_ffn = _rec_inputs()

    def _L0_xattn_setup():
        import jax, jax.numpy as jnp
        import numpy as np
        from jax import lax
        BIG = jnp.float32(1e+30)

        def _pairwise_euclidean(a, b):
            aa = jnp.sum(a * a, axis=-1)[:, None]
            bb = jnp.sum(b * b, axis=-1)[None, :]
            ab = a @ b.T
            return jnp.sqrt(jnp.maximum(aa + bb - 2.0 * ab, 0.0))

        def _dtw_cost(D):
            row0 = jnp.cumsum(D[0])

            def row_step(prev_row, d_row):
                first = d_row[0] + prev_row[0]

                def col_step(left, inp):
                    d_ij, up, diag = inp
                    r = d_ij + jnp.minimum(jnp.minimum(up, left), diag)
                    return (r, r)
                _, rest = lax.scan(col_step, first, (d_row[1:], prev_row[1:], prev_row[:-1]))
                row = jnp.concatenate([first[None], rest])
                return (row, row)
            _, rows = lax.scan(row_step, row0, D[1:])
            return jnp.concatenate([row0[None], rows], axis=0)

        def _backtrack(R, T1, T2):
            L = T1 + T2 - 1

            def step(carry, _):
                i, j, done = carry
                valid = jnp.logical_not(done)
                cd = jnp.where((i > 0) & (j > 0), R[jnp.maximum(i - 1, 0), jnp.maximum(j - 1, 0)], BIG)
                cu = jnp.where(i > 0, R[jnp.maximum(i - 1, 0), j], BIG)
                cl = jnp.where(j > 0, R[i, jnp.maximum(j - 1, 0)], BIG)
                choice = jnp.argmin(jnp.stack([cd, cu, cl]))
                ni = jnp.where(choice <= 1, i - 1, i)
                nj = jnp.where((choice == 0) | (choice == 2), j - 1, j)
                at_origin = (i == 0) & (j == 0)
                ni = jnp.where(at_origin, 0, ni)
                nj = jnp.where(at_origin, 0, nj)
                return ((ni, nj, done | at_origin), (i, j, valid))
            init = (jnp.int32(T1 - 1), jnp.int32(T2 - 1), jnp.bool_(False))
            _, (i_idx, j_idx, valid) = lax.scan(step, init, None, length=L)
            return (i_idx, j_idx, valid)

        def _align_one(small, large):
            T_small, d = small.shape
            T_large = large.shape[0]
            D = _pairwise_euclidean(small, large)
            R = _dtw_cost(D)
            i_idx, j_idx, valid = _backtrack(R, T_small, T_large)
            contrib = small[i_idx] * valid[:, None].astype(small.dtype)
            expanded = jnp.zeros((T_large, d), dtype=small.dtype).at[j_idx].add(contrib)
            return expanded
        key = jax.random.key(seed)
        k1, k2 = jax.random.split(key)
        teacher = jax.random.normal(k1, (16, 50, 128), dtype=jnp.float32)
        student = jax.random.normal(k2, (16, 75, 128), dtype=jnp.float32)
        return {'teacher_features': teacher, 'student_features': student}
    _L0_xattn_all = _L0_xattn_setup()
    _L0_xattn_in = {k: v for k, v in _L0_xattn_all.items() if k in ()}
    del _L0_xattn_all

    def _L0_ffn_setup():
        import jax, jax.numpy as jnp
        import numpy as np
        B, S, H, E, I, MAX_K, A_HID = (2, 256, 128, 8, 336, 6, 50)
        key = jax.random.key(seed)
        ks = jax.random.split(key, 10)
        sc = 0.02
        return {'hidden_states': jax.random.normal(ks[0], (B, S, H), dtype=jnp.float32), 'router_w': jax.random.normal(ks[1], (E, H), dtype=jnp.float32) * sc, 'actor_w1': jax.random.normal(ks[2], (A_HID, H), dtype=jnp.float32) * sc, 'actor_b1': jnp.zeros((A_HID,), dtype=jnp.float32), 'actor_w2': jax.random.normal(ks[3], (MAX_K, A_HID), dtype=jnp.float32) * sc, 'actor_b2': jnp.zeros((MAX_K,), dtype=jnp.float32), 'gate_w': jax.random.normal(ks[4], (E, I, H), dtype=jnp.float32) * sc, 'up_w': jax.random.normal(ks[5], (E, I, H), dtype=jnp.float32) * sc, 'down_w': jax.random.normal(ks[6], (E, H, I), dtype=jnp.float32) * sc}
    _L0_ffn_all = _L0_ffn_setup()
    _L0_ffn_in = {k: v for k, v in _L0_ffn_all.items() if k in ('router_w', 'actor_w1', 'actor_b1', 'actor_w2', 'actor_b2', 'gate_w', 'up_w', 'down_w')}
    del _L0_ffn_all
    return {'x': x, 'ctx_1024': ctx_1024, 'g_xattn': g_xattn, 'g_ffn': g_ffn, 'L0_ffn_router_w': _L0_ffn_in['router_w'], 'L0_ffn_actor_w1': _L0_ffn_in['actor_w1'], 'L0_ffn_actor_b1': _L0_ffn_in['actor_b1'], 'L0_ffn_actor_w2': _L0_ffn_in['actor_w2'], 'L0_ffn_actor_b2': _L0_ffn_in['actor_b2'], 'L0_ffn_gate_w': _L0_ffn_in['gate_w'], 'L0_ffn_up_w': _L0_ffn_in['up_w'], 'L0_ffn_down_w': _L0_ffn_in['down_w']}

def reference(x, ctx_1024, g_xattn, g_ffn, L0_ffn_router_w, L0_ffn_actor_w1, L0_ffn_actor_b1, L0_ffn_actor_w2, L0_ffn_actor_b2, L0_ffn_gate_w, L0_ffn_up_w, L0_ffn_down_w):
    import jax
    import jax.numpy as jnp

    def _L0_xattn_ref(teacher_features, student_features):
        import jax, jax.numpy as jnp
        import numpy as np
        from jax import lax
        BIG = jnp.float32(1e+30)

        def _pairwise_euclidean(a, b):
            aa = jnp.sum(a * a, axis=-1)[:, None]
            bb = jnp.sum(b * b, axis=-1)[None, :]
            ab = a @ b.T
            return jnp.sqrt(jnp.maximum(aa + bb - 2.0 * ab, 0.0))

        def _dtw_cost(D):
            row0 = jnp.cumsum(D[0])

            def row_step(prev_row, d_row):
                first = d_row[0] + prev_row[0]

                def col_step(left, inp):
                    d_ij, up, diag = inp
                    r = d_ij + jnp.minimum(jnp.minimum(up, left), diag)
                    return (r, r)
                _, rest = lax.scan(col_step, first, (d_row[1:], prev_row[1:], prev_row[:-1]))
                row = jnp.concatenate([first[None], rest])
                return (row, row)
            _, rows = lax.scan(row_step, row0, D[1:])
            return jnp.concatenate([row0[None], rows], axis=0)

        def _backtrack(R, T1, T2):
            L = T1 + T2 - 1

            def step(carry, _):
                i, j, done = carry
                valid = jnp.logical_not(done)
                cd = jnp.where((i > 0) & (j > 0), R[jnp.maximum(i - 1, 0), jnp.maximum(j - 1, 0)], BIG)
                cu = jnp.where(i > 0, R[jnp.maximum(i - 1, 0), j], BIG)
                cl = jnp.where(j > 0, R[i, jnp.maximum(j - 1, 0)], BIG)
                choice = jnp.argmin(jnp.stack([cd, cu, cl]))
                ni = jnp.where(choice <= 1, i - 1, i)
                nj = jnp.where((choice == 0) | (choice == 2), j - 1, j)
                at_origin = (i == 0) & (j == 0)
                ni = jnp.where(at_origin, 0, ni)
                nj = jnp.where(at_origin, 0, nj)
                return ((ni, nj, done | at_origin), (i, j, valid))
            init = (jnp.int32(T1 - 1), jnp.int32(T2 - 1), jnp.bool_(False))
            _, (i_idx, j_idx, valid) = lax.scan(step, init, None, length=L)
            return (i_idx, j_idx, valid)

        def _align_one(small, large):
            T_small, d = small.shape
            T_large = large.shape[0]
            D = _pairwise_euclidean(small, large)
            R = _dtw_cost(D)
            i_idx, j_idx, valid = _backtrack(R, T_small, T_large)
            contrib = small[i_idx] * valid[:, None].astype(small.dtype)
            expanded = jnp.zeros((T_large, d), dtype=small.dtype).at[j_idx].add(contrib)
            return expanded
        return jax.vmap(_align_one)(teacher_features, student_features)

    def _L0_ffn_ref(hidden_states, router_w, actor_w1, actor_b1, actor_w2, actor_b2, gate_w, up_w, down_w):
        import jax, jax.numpy as jnp
        import numpy as np
        B, S, H, E, I, MAX_K, A_HID = (2, 256, 128, 8, 336, 6, 50)
        probs = jax.nn.softmax(jnp.einsum('bsh,eh->bse', hidden_states, router_w).astype(jnp.float32), axis=-1)
        a_h = jax.nn.gelu(jnp.einsum('bsh,ah->bsa', hidden_states, actor_w1) + actor_b1)
        actor_logits = jnp.clip(jnp.einsum('bsa,ka->bsk', a_h, actor_w2) + actor_b2, -30.0, 30.0)
        sampled_k = jnp.argmax(actor_logits, axis=-1) + 1
        order = jnp.argsort(-probs, axis=-1)
        rank = jnp.argsort(order, axis=-1)
        mask = rank < sampled_k[..., None]
        scores = jnp.where(mask, probs, 0.0).astype(hidden_states.dtype)
        out = jnp.zeros_like(hidden_states)
        for e in range(E):
            g = jnp.einsum('bsh,ih->bsi', hidden_states, gate_w[e])
            u = jnp.einsum('bsh,ih->bsi', hidden_states, up_w[e])
            y = jnp.einsum('bsi,hi->bsh', jax.nn.silu(g) * u, down_w[e])
            out = out + scores[..., e:e + 1] * y
        return out
    x = x + jnp.tanh(g_xattn[0]) * _L0_xattn_ref(ctx_1024, _layernorm(x, axis=-1))
    x = x + jnp.tanh(g_ffn[0]) * _L0_ffn_ref(_layernorm(x, axis=-1), L0_ffn_router_w, L0_ffn_actor_w1, L0_ffn_actor_b1, L0_ffn_actor_w2, L0_ffn_actor_b2, L0_ffn_gate_w, L0_ffn_up_w, L0_ffn_down_w)
    return x

_drawn_inputs = setup_inputs


def setup_inputs(seed=0):
    import zlib

    import numpy as np

    out = dict(_drawn_inputs(seed))
    spreads = {'L0_ffn_actor_b1': (0.0, 0.8), 'L0_ffn_actor_b2': (0.0, 0.8)}
    factors = {'L0_ffn_router_w': 8.0,
     'L0_ffn_actor_w1': 8.0,
     'L0_ffn_actor_w2': 8.0,
     'L0_ffn_gate_w': 8.0,
     'L0_ffn_up_w': 8.0,
     'L0_ffn_down_w': 8.0}
    for name, (base, spread) in spreads.items():
        noise = np.random.default_rng([zlib.crc32(name.encode()), seed]).standard_normal(out[name].shape)
        drawn = base * np.exp(spread * noise) if base else spread * noise
        out[name] = jnp.asarray(drawn.astype(out[name].dtype))
    for name, factor in factors.items():
        out[name] = (out[name] * factor).astype(out[name].dtype)
    return out
```

```python
from contextlib import ExitStack

import concourse.bass as bass
from concourse import mybir

BATCH, ROWS, DIM = 4, 256, 128
EXPERTS, INNER, MAX_K, ACTOR = 8, 336, 6, 50
P = 128
TILES = BATCH * ROWS // P
HALVES = ROWS // P
LANE_COLS = 16
LANES = ROWS // LANE_COLS
QUAD = 32
LAG = 2
GROUP = 8
RING = 4 * GROUP
STEPS = 288
GROUPS = STEPS // GROUP
TURNS = STEPS // RING
BLOCK = 8
BLOCKS = ROWS // BLOCK
CHUNK_ENDS = [96, 192, 240, 256]
SKEW = LAG * (LANES - 1)
D_WIDTH = ROWS + 2 * SKEW + 4
M_PAD = 32
M_WIDTH = STEPS + M_PAD + 8
SUB = 112
SUBS = INNER // SUB
HALF_TOKENS = BATCH * P
FAR = 1e30
LABEL = 1.0 / 1024

C_IDENT, C_DIAG, C_BATCH, C_EARLIER, C_ORDER, C_FIRST = 0, 128, 160, 288, 352, 360
C_WIDTH = 361
H_IDENT, H_LABEL, H_TWICE, H_TWICE2, H_TWICE4 = 0, 128, 384, 640, 896
H_WIDTH = 1152


def build(nc, x_tok, ctx_t, ctx_blk, gates, w_gate, w_up, w_down, w_router, w_a1, b_a1, w_a2, b_a2,
          const32, const16, dist_dram, mask_dram, out):
    F32, F16, F32R = mybir.dt.float32, mybir.dt.float16, mybir.dt.float32r
    ALU, ACT, AX = mybir.AluOpType, mybir.ActivationFunctionType, mybir.AxisListType

    with ExitStack() as stack:
        def sb(name, shape, dtype=F32):
            return stack.enter_context(nc.sbuf_tensor(name, shape, dtype))

        def sem(name):
            return stack.enter_context(nc.semaphore(name))

        x = sb("x", [P, TILES, DIM])
        ctxb = sb("ctxb", [P, BLOCK, DIM])
        c32 = sb("c32", [P, C_WIDTH])
        c16 = sb("c16", [P, H_WIDTH], F16)
        ones = sb("ones", [P, P])
        gin = sb("gin", [1, 2])
        tg = sb("tg", [P, 2])
        stats = sb("stats", [P, TILES, 6])
        mv = sb("mv", [P, TILES, 2])
        var = sb("var", [P, TILES])
        std = sb("std", [P, TILES])
        rstd = sb("rstd", [P, TILES])
        xn = sb("xn", [P, TILES, DIM])
        bb = sb("bb", [P, TILES])
        KT = sb("KT", [P, HALVES, 2, BATCH, ROWS], F16)
        entry = sb("entry", [BATCH, BLOCKS])
        gu_hi = sb("gu_hi", [P, EXPERTS, 2, INNER], F32R)
        gu_lo = sb("gu_lo", [P, EXPERTS, 2, INNER], F32R)
        dn_hi = sb("dn_hi", [SUB, EXPERTS, SUBS * DIM], F32R)
        dn_lo = sb("dn_lo", [SUB, EXPERTS, SUBS * DIM], F32R)
        wr = sb("wr", [P, EXPERTS])
        wa1 = sb("wa1", [P, ACTOR])
        ba1 = sb("ba1", [ACTOR, 1])
        wa2 = sb("wa2", [ACTOR, MAX_K])
        ba2 = sb("ba2", [1, MAX_K])

        early = ExitStack()

        def sb(name, shape, dtype=F32):
            return early.enter_context(nc.sbuf_tensor(name, shape, dtype))

        ctxT = sb("ctxT", [P, BATCH * ROWS])
        ctxsq = sb("ctxsq", [P, BATCH * ROWS])
        sq_junk = sb("sq_junk", [P, DIM])
        xnT = sb("xnT", [P, TILES * P])
        DT = sb("DT", [P, TILES, D_WIDTH])
        Dk = sb("Dk", [P, LANE_COLS, STEPS])
        Dring = sb("Dring", [P, RING, LANE_COLS])
        ring = sb("ring", [P, RING, LANE_COLS + 1])
        mring = sb("mring", [P, RING, LANE_COLS])
        diff = sb("diff", [P, 2, 2, GROUP, LANE_COLS])
        K = sb("K", [P, LANE_COLS, 2, STEPS + 2], F16)
        gu_w = sb("gu_w", [P, EXPERTS, 2, INNER])
        dn_w = sb("dn_w", [SUB, EXPERTS, SUBS * DIM])
        early.close()

        def sb(name, shape, dtype=F32):
            return stack.enter_context(nc.sbuf_tensor(name, shape, dtype))

        notleft = sb("notleft", [P, BLOCK, ROWS], F16)
        up = sb("up", [P, BLOCK, ROWS], F16)
        exit2 = sb("exit2", [P, BLOCK, ROWS], F16)
        upsum = sb("upsum", [P, BLOCK, ROWS], F16)
        lab = sb("lab", [P, 2, ROWS + 1], F16)
        lab_t = sb("lab_t", [P, ROWS], F16)
        lab_e = sb("lab_e", [P, ROWS], F16)
        block_map = sb("block_map", [BATCH, BLOCKS, ROWS], F16)
        junk = sb("junk", [P, ROWS])
        entry0 = sb("entry0", [P, 1])
        junk32 = sb("junk32", [P, BLOCKS])
        within = sb("within", [P, BLOCK, ROWS], F16)
        q = sb("q", [P, BLOCK])
        path = sb("path", [P, BLOCK, ROWS])
        x1 = sb("x1", [P, TILES, DIM])
        xT = sb("xT", [P, TILES * P])
        xT_hi = sb("xT_hi", [P, TILES * P], F32R)
        xT_lo = sb("xT_lo", [P, TILES * P], F32R)
        actor = sb("actor", [ACTOR, TILES * P])
        logit = sb("logit", [P, TILES, EXPERTS])
        shifted = sb("shifted", [P, TILES, EXPERTS])
        prob = sb("prob", [P, TILES, EXPERTS])
        tile1 = [sb(f"tile1_{i}", [P, TILES]) for i in range(6)]
        pair = sb("pair", [P, TILES, EXPERTS, EXPERTS])
        pair2 = sb("pair2", [P, TILES, EXPERTS, EXPERTS])
        rank = sb("rank", [P, TILES, EXPERTS])
        choice = sb("choice", [P, TILES, MAX_K])
        first = sb("first", [P, TILES, MAX_K])
        score = sb("score", [P, TILES, EXPERTS])
        silu = sb("silu", [SUB, 2, HALF_TOKENS])
        act = sb("act", [SUB, 2, HALF_TOKENS])
        act_hi = sb("act_hi", [SUB, 2 * SUBS, HALF_TOKENS], F32R)
        act_lo = sb("act_lo", [SUB, 2 * SUBS, HALF_TOKENS], F32R)
        acc = sb("acc", [P, TILES, DIM])
        bank = [stack.enter_context(nc.psum_tensor(f"bank{i}", [P, 512], F32)) for i in range(8)]

        x_in, ctx_in, c32_in, c16_in, ctxb_in = map(sem, ("x_in", "ctx_in", "c32_in", "c16_in", "ctxb_in"))
        gates_in, weights_in, router_in = map(sem, ("gates_in", "weights_in", "router_in"))
        cleared = sem("cleared")
        ring_clear = sem("ring_clear")
        dve_step = sem("dve_step")
        var_ready, std_ready, xn_ready = map(sem, ("var_ready", "std_ready", "xn_ready"))
        bb_ready, xnT_psum, xnT_ready, ctxsq_ready = map(sem, ("bb_ready", "xnT_psum", "xnT_ready", "ctxsq_ready"))
        gate_psum, gate_ready = map(sem, ("gate_psum", "gate_ready"))
        dot_psum, sqdist_ready, dist_ready = map(sem, ("dot_psum", "sqdist_ready", "dist_ready"))
        dist_stored, lanes_in = sem("dist_stored"), sem("lanes_in")
        masks_stored = sem("masks_stored")
        dring_ready = sem("dring_ready")
        sweep = sem("sweep")
        diff_ready = sem("diff_ready")
        signs_ready = sem("signs_ready")
        masks_moved = sem("masks_moved")
        w_hi_ready, w_lo_ready = sem("w_hi_ready"), sem("w_lo_ready")
        masks_psum, notleft_ready, up_ready, exit_ready = map(sem, ("masks_psum", "notleft_ready", "up_ready", "exit_ready"))
        up_label_ready, upsum_ready = sem("up_label_ready"), sem("upsum_ready")
        labels_ready, map_moved, entries_ready = map(sem, ("labels_ready", "map_moved", "entries_ready"))
        entry_psum, path_ready, attn_psum, x1_ready = map(sem, ("entry_psum", "path_ready", "attn_psum", "x1_ready"))
        var2_ready, std2_ready, xn2_ready = map(sem, ("var2_ready", "std2_ready", "xn2_ready"))
        xT_psum, xT_ready, xT_hi_ready, xT_lo_ready = map(sem, ("xT_psum", "xT_ready", "xT_hi_ready", "xT_lo_ready"))
        router_psum, actor_psum, actor_ready, choice_psum = map(sem, ("router_psum", "actor_psum", "actor_ready", "choice_psum"))
        shifted_ready, exp_ready = sem("shifted_ready"), sem("exp_ready")
        gu_psum, silu_ready, act_ready, act_hi_ready, act_lo_ready = map(
            sem, ("gu_psum", "silu_ready", "act_ready", "act_hi_ready", "act_lo_ready"))
        down_psum, acc_ready, out_done = map(sem, ("down_psum", "acc_ready", "out_done"))
        stack.enter_context(nc.allow_non_contiguous_dma(reason="single columns of small operands"))
        block = stack.enter_context(nc.Block())

        ident = c32[:, C_IDENT:C_IDENT + P]
        ident16 = c16[:, H_IDENT:H_IDENT + P]

        def half16(t, at):
            return t[:, at:at + ROWS]

        units = [(h, e) for h in range(HALVES) for e in range(EXPERTS)]

        @block.sync
        def _(sp):
            sp.dma_start(x[:], x_tok).then_inc(x_in, 16)
            sp.dma_start(c32[:], const32).then_inc(c32_in, 16)
            sp.dma_start(gin[:], gates).then_inc(gates_in, 16)
            for h in range(HALVES):
                sp.wait_ge(dist_ready, BATCH * (h + 1))
                sp.dma_start(bass.AP(dist_dram.tensor, h * P * D_WIDTH,
                                     [[D_WIDTH, P], [ROWS * D_WIDTH, BATCH], [1, D_WIDTH]]),
                             DT[:, h * BATCH:(h + 1) * BATCH, :]).then_inc(dist_stored, 16)
            sp.wait_ge(dist_stored, 16 * HALVES)
            sp.wait_ge(cleared, 1)
            for b in range(BATCH):
                src = bass.AP(dist_dram.tensor, b * ROWS * D_WIDTH + SKEW,
                              [[LANE_COLS * D_WIDTH - LAG, LANES], [D_WIDTH, LANE_COLS], [1, STEPS]])
                sp.dma_start(Dk[b * QUAD:b * QUAD + LANES, :, :], src).then_inc(lanes_in, 16)
            begin, sent = 0, 0
            for chunk, end in enumerate(CHUNK_ENDS):
                groups = -(-(end + SKEW) // GROUP)
                upto = groups * GROUP + 1
                sp.wait_ge(signs_ready, 2 * groups)
                for b in range(BATCH):
                    dst = bass.AP(mask_dram.tensor, b * 2 * ROWS * M_WIDTH + sent + M_PAD - 1,
                                  [[2 * LANE_COLS * M_WIDTH - LAG, LANES], [M_WIDTH, 2 * LANE_COLS],
                                   [1, upto - sent]])
                    sp.dma_start(dst, K[b * QUAD:b * QUAD + LANES, :, :, sent:upto]
                                 .rearrange("c j m t -> c (j m) t")).then_inc(masks_stored, 16)
                sp.wait_ge(masks_stored, 16 * BATCH * (chunk + 1))
                for h in range(HALVES):
                    for plane in range(2):
                        src = bass.AP(mask_dram.tensor, (h * P * 2 + plane) * M_WIDTH + M_PAD + begin,
                                      [[2 * M_WIDTH, P], [2 * ROWS * M_WIDTH, BATCH], [1, end - begin]])
                        sp.dma_start(KT[:, h, plane, :, begin:end], src).then_inc(masks_moved, 16)
                begin, sent = end, upto
            sp.wait_ge(labels_ready, 1)
            for b in range(BATCH):
                sp.dma_start(block_map[b:b + 1, :, :], lab[b * BLOCKS:(b + 1) * BLOCKS, 0, 1:ROWS + 1])\
                  .then_inc(map_moved, 16)
            for h in range(HALVES):
                sp.wait_ge(acc_ready, BATCH * EXPERTS * (h + 1))
                sp.dma_start(out[:, h], acc[:, h * BATCH:(h + 1) * BATCH, :]).then_inc(out_done, 16)
            sp.wait_ge(out_done, 16 * HALVES)

        @block.gpsimd
        def _(pool):
            nc.gpsimd.memset(Dk[:], FAR).then_inc(cleared, 1)
            nc.gpsimd.memset(ones[:], 1.0).then_inc(cleared, 1)
            nc.gpsimd.memset(K[:, :, :, 0:2], 0.0).then_inc(cleared, 1)

            def group_diffs(q_, group, head):
                s = q_ * GROUP
                pool.wait_ge(sweep, 3 * GROUP * (group + 1))
                if not head or q_ >= 2:
                    pool.wait_ge(signs_ready, group * 2 - 2)
                left = ring[:, s:s + GROUP, 0:LANE_COLS]
                nc.gpsimd.tensor_tensor(out=diff[:, q_ % 2, 0], in0=left, in1=mring[:, s:s + GROUP, :],
                                        op=ALU.subtract).then_inc(diff_ready, 1)
                nc.gpsimd.tensor_tensor(out=diff[:, q_ % 2, 1], in0=left, in1=ring[:, s:s + GROUP, 1:LANE_COLS + 1],
                                        op=ALU.subtract).then_inc(diff_ready, 1)

            for q_ in range(4):
                group_diffs(q_, q_, True)
            with pool.Fori(1, TURNS) as k:
                for q_ in range(4):
                    group_diffs(q_, k * 4 + q_, False)
                pool.wait_ge(w_hi_ready, k * 2)
                nc.gpsimd.tensor_tensor(out=gu_lo[:, bass.ds(k - 1, 1)], in0=gu_w[:, bass.ds(k - 1, 1)],
                                        in1=gu_hi[:, bass.ds(k - 1, 1)].bitcast(F32), op=ALU.subtract)\
                    .then_inc(w_lo_ready, 1)
                nc.gpsimd.tensor_tensor(out=dn_lo[:, bass.ds(k - 1, 1)], in0=dn_w[:, bass.ds(k - 1, 1)],
                                        in1=dn_hi[:, bass.ds(k - 1, 1)].bitcast(F32), op=ALU.subtract)\
                    .then_inc(w_lo_ready, 1)
            pool.wait_ge(up_label_ready, 1)
            pool.wait_ge(c16_in, 16)
            nc.gpsimd.tensor_tensor(out=upsum[:], in0=upsum[:],
                                    in1=half16(c16, H_TWICE2).unsqueeze(1).to_broadcast([P, BLOCK, ROWS]),
                                    op=ALU.add).then_inc(upsum_ready, 1)
            pool.wait_ge(upsum_ready, 1)
            pool.wait_ge(notleft_ready, BLOCK // 2)
            nc.gpsimd.tensor_tensor(out=exit2[:], in0=upsum[:], in1=notleft[:], op=ALU.mult).then_inc(exit_ready, 1)

        @block.scalar
        def _(sc):
            sc.dma_start(ctxT[:], ctx_t).then_inc(ctx_in, 16)
            sc.dma_start(c16[:], const16).then_inc(c16_in, 16)
            sc.dma_start(ctxb[:], ctx_blk).then_inc(ctxb_in, 16)
            sc.dma_start(gu_w[:, :, 0, :], w_gate).then_inc(weights_in, 16)
            sc.dma_start(gu_w[:, :, 1, :], w_up).then_inc(weights_in, 16)
            sc.dma_start(dn_w[:], w_down).then_inc(weights_in, 16)
            for dst, src in ((wr, w_router), (wa1, w_a1), (ba1, b_a1), (wa2, w_a2), (ba2, b_a2)):
                sc.dma_start(dst[:], src).then_inc(router_in, 16)
            sc.wait_ge(gate_psum, 1)
            nc.scalar.activation(tg[:], bank[6][:, 0:2], ACT.Tanh).then_inc(gate_ready, 1)
            sc.wait_ge(var_ready, 1)
            nc.scalar.activation(std[:], var[:], ACT.Sqrt).then_inc(std_ready, 1)
            for n in range(TILES):
                sc.wait_ge(xn_ready, n + 1)
                if n:
                    sc.wait_ge(bb_ready, n)
                nc.scalar.activation(sq_junk[:], xn[:, n, :], ACT.Square, accum_out=bb[:, n:n + 1]).then_inc(bb_ready, 1)
            sc.wait_ge(xnT_psum, TILES)
            nc.scalar.activation(xnT[:, 512:1024], bank[1][:], ACT.Copy).then_inc(xnT_ready, 1)
            for n in range(TILES):
                sc.wait_ge(sqdist_ready, n + 1)
                nc.scalar.activation(DT[:, n, SKEW:SKEW + ROWS], DT[:, n, SKEW:SKEW + ROWS], ACT.Sqrt).then_inc(dist_ready, 1)

            def dist_group(slot, group_start):
                nc.scalar.activation(Dring[:, slot * GROUP:(slot + 1) * GROUP, :].rearrange("p t j -> p j t"),
                                     Dk[:, :, group_start], ACT.Copy).then_inc(dring_ready, 1)

            def sign_group(half, own, after):
                for plane, cols in ((0, own), (1, after)):
                    nc.scalar.activation(K[:, :, plane, cols], diff[:, half, plane].rearrange("p t j -> p j t"), ACT.Sign)\
                        .then_inc(signs_ready, 1)

            sc.wait_ge(lanes_in, 16 * BATCH)
            for g in range(4):
                dist_group(g, slice(g * GROUP, (g + 1) * GROUP))
            sc.wait_ge(weights_in, 48)
            sc.wait_ge(cleared, 3)
            with sc.Fori(0, TURNS - 1) as k:
                for s in range(4):
                    sc.wait_ge(sweep, k * (12 * GROUP) + 3 * GROUP * (s + 1))
                    dist_group(s, bass.ds(k * RING + (RING + s * GROUP), GROUP))
                    sc.wait_ge(diff_ready, k * 8 + 2 * (s + 1))
                    sign_group(s % 2, bass.ds(k * RING + (s * GROUP + 1), GROUP), bass.ds(k * RING + (s * GROUP + 2), GROUP))
                nc.scalar.activation(gu_hi[:, bass.ds(k, 1)], gu_w[:, bass.ds(k, 1)], ACT.Copy).then_inc(w_hi_ready, 1)
                nc.scalar.activation(dn_hi[:, bass.ds(k, 1)], dn_w[:, bass.ds(k, 1)], ACT.Copy).then_inc(w_hi_ready, 1)
            for g in range(GROUPS - 4, GROUPS):
                sc.wait_ge(diff_ready, 2 * (g + 1))
                sign_group(g % 2, slice(g * GROUP + 1, (g + 1) * GROUP + 1), slice(g * GROUP + 2, (g + 1) * GROUP + 2))
            for pr in range(BLOCK // 2):
                sc.wait_ge(masks_psum, 2 * (pr + 1))
                src = bank[4 + pr][:].bitcast(F16)[:, 0:2 * ROWS].rearrange("p (r j) -> p r j", r=2)
                nc.scalar.activation(up[:, 2 * pr:2 * pr + 2, :], src, ACT.Relu).then_inc(up_ready, 1)
            sc.wait_ge(up_ready, BLOCK // 2)
            nc.scalar.activation(upsum[:], up[:], ACT.Copy, scale=LABEL).then_inc(up_label_ready, 1)
            sc.wait_ge(var2_ready, 1)
            nc.scalar.activation(std[:], var[:], ACT.Sqrt).then_inc(std2_ready, 1)
            for h in range(HALVES):
                sc.wait_ge(xT_ready, h + 1)
                nc.scalar.activation(xT_hi[:, h * 512:(h + 1) * 512], xT[:, h * 512:(h + 1) * 512], ACT.Copy).then_inc(xT_hi_ready, 1)

            def silu_tile(v):
                sc.wait_ge(gu_psum, v + 1)
                if v >= 2:
                    sc.wait_ge(act_ready, v - 1)
                nc.scalar.activation(silu[:, v % 2, :], bank[v % 2][0:SUB, :], ACT.Silu).then_inc(silu_ready, 1)

            def high_part(v):
                sc.wait_ge(act_ready, v + 1)
                if v >= 2 * SUBS:
                    sc.wait_ge(down_psum, v // SUBS - 1)
                nc.scalar.activation(act_hi[:, v % (2 * SUBS), :], act[:, v % 2, :], ACT.Copy).then_inc(act_hi_ready, 1)

            total = len(units) * SUBS
            for v in range(total):
                silu_tile(v)
                if v:
                    high_part(v - 1)
                if v == 1:
                    for h in range(HALVES):
                        sc.wait_ge(actor_psum, h + 1)
                        sc.wait_ge(router_in, 80)
                        nc.scalar.activation(actor[:, h * 512:(h + 1) * 512], bank[7][0:ACTOR, :], ACT.Gelu_apprx_tanh,
                                             bias=ba1[:, 0:1]).then_inc(actor_ready, 1)
                    sc.wait_ge(shifted_ready, 1)
                    nc.scalar.activation(prob[:], shifted[:], ACT.Exp).then_inc(exp_ready, 1)
            high_part(total - 1)

        @block.vector
        def _(dve):
            steps = [0]

            def link(ins):
                steps[0] += 1
                ins.then_inc(dve_step, 1)
                dve.wait_ge(dve_step, steps[0])

            def norm(src, own, dst, var_sem, std_sem, out_sem):
                for n in range(TILES):
                    nc.vector.bn_stats(stats[:, n, :], src[:, n, :]).then_inc(dve_step, 1)
                steps[0] += TILES
                dve.wait_ge(dve_step, steps[0])
                for n in range(TILES):
                    nc.vector.bn_aggr(mv[:, n, :], stats[:, n, :]).then_inc(dve_step, 1)
                steps[0] += TILES
                dve.wait_ge(dve_step, steps[0])
                nc.vector.tensor_scalar(var[:], mv[:, :, 1], 1e-5, None, ALU.add).then_inc(var_sem, 1)
                dve.wait_ge(std_sem, 1)
                link(nc.vector.reciprocal(rstd[:], std[:]))
                for n in range(TILES):
                    nc.vector.tensor_scalar(dst[:, n, :], src[:, n, :], mv[:, n, 0:1], rstd[:, n:n + 1],
                                            ALU.subtract, ALU.mult).then_inc(out_sem, 1)

            nc.vector.memset(ring[:], FAR).then_inc(ring_clear, 1)
            nc.vector.memset(DT[:], FAR).then_inc(ring_clear, 1)
            dve.wait_ge(x_in, 16)
            norm(x, None, xn, var_ready, std_ready, xn_ready)
            dve.wait_ge(ctx_in, 16)
            nc.vector.scalar_tensor_tensor(out=ctxsq[:], in0=ctxT[:], scalar=-0.5, in1=ctxT[:], op0=ALU.mult,
                                           op1=ALU.mult).then_inc(ctxsq_ready, 1)
            dve.wait_ge(xnT_psum, TILES // 2)
            nc.vector.tensor_copy(xnT[:, 0:512], bank[0][:]).then_inc(xnT_ready, 1)
            dve.wait_ge(ring_clear, 2)
            for n in range(TILES):
                dve.wait_ge(dot_psum, n // 2 * 2 + 2)
                dve.wait_ge(bb_ready, n + 1)
                link(nc.vector.tensor_scalar(DT[:, n, SKEW:SKEW + ROWS], bank[2 + n // 2][:, (n % 2) * ROWS:(n % 2 + 1) * ROWS],
                                             -2.0, bb[:, n:n + 1], ALU.mult, ALU.add))
                nc.vector.tensor_scalar(DT[:, n, SKEW:SKEW + ROWS], DT[:, n, SKEW:SKEW + ROWS], 0.0, None, ALU.max).then_inc(sqdist_ready, 1)

            quarter = list(range(QUAD))
            mask = [QUAD - 1] + quarter[:-1]

            def sweep_step(u, base, group, head):
                before = (u - 1) % RING
                if u % GROUP == GROUP - 1 and (not head or u == RING - 1):
                    dve.wait_ge(diff_ready, group * 2 - 4)
                if head and u == 0:
                    dve.wait_ge(ring_clear, 2)
                    dve.wait_ge(c32_in, 16)
                else:
                    dve.wait_ge(sweep, base)
                nc.vector.tensor_tensor(out=mring[:, u, :], in0=ring[:, before, 0:LANE_COLS],
                                        in1=ring[:, before, 1:LANE_COLS + 1], op=ALU.min).then_inc(sweep, 1)
                nc.vector.stream_shuffle(out=ring[:, (u + 1) % RING, 0:1], in_=ring[:, before, LANE_COLS:LANE_COLS + 1],
                                         mask=mask).then_inc(sweep, 1)
                if u % GROUP == 0:
                    dve.wait_ge(dring_ready, group + 1)
                dve.wait_ge(sweep, base + 1)
                halo = c32[:, C_FIRST:C_FIRST + 1] if head and u == 0 else ring[:, u, 0:1]
                nc.vector.tensor_tensor_scan(out=ring[:, u, 1:LANE_COLS + 1], data0=mring[:, u, :],
                                             data1=Dring[:, u, :], initial=halo, op0=ALU.min, op1=ALU.add)\
                    .then_inc(sweep, 1)

            for u in range(RING):
                sweep_step(u, 3 * u, u // GROUP, True)
            with dve.Fori(1, TURNS) as k:
                for u in range(RING):
                    sweep_step(u, k * (3 * RING) + 3 * u, k * 4 + u // GROUP, False)

            dve.wait_ge(w_lo_ready, 2 * EXPERTS)
            link(nc.vector.memset(lab[:, :, 0:1], 0.0))
            link(nc.vector.memset(entry[:, BLOCKS - 1:BLOCKS], (2 * ROWS - 1) * LABEL))
            for pr in range(BLOCK // 2):
                dve.wait_ge(masks_psum, 2 * (pr + 1))
                src = bank[pr][:].bitcast(F16)[:, 0:2 * ROWS].rearrange("p (r j) -> p r j", r=2)
                nc.vector.tensor_scalar(notleft[:, 2 * pr:2 * pr + 2, :], src, 0.0, None, ALU.is_ge)\
                    .then_inc(notleft_ready, 1)
            dve.wait_ge(c16_in, 16)
            link(nc.vector.tensor_copy(lab[:, 0, 1:ROWS + 1], half16(c16, H_LABEL)))
            for r in range(BLOCK):
                src, dst = lab[:, r % 2], lab[:, (r + 1) % 2]
                if r % 2 == 0:
                    dve.wait_ge(up_ready, r // 2 + 1)
                    dve.wait_ge(notleft_ready, r // 2 + 1)
                link(nc.vector.tensor_tensor(out=lab_t[:], in0=src[:, 1:ROWS + 1], in1=up[:, r, :], op=ALU.min))
                link(nc.vector.tensor_tensor(out=lab_e[:], in0=lab_t[:], in1=src[:, 0:ROWS], op=ALU.max))
                scan = nc.vector.tensor_tensor_scan(out=dst[:, 1:ROWS + 1], data0=notleft[:, r, :], data1=lab_e[:],
                                                    initial=0.0, op0=ALU.max, op1=ALU.min)
                if r < BLOCK - 1:
                    link(scan)
                else:
                    scan.then_inc(labels_ready, 1)
            dve.wait_ge(map_moved, 16 * BATCH)
            for k in range(BLOCKS - 1, 0, -1):
                if k < BLOCKS - 1:
                    dve.wait_ge(entries_ready, BLOCKS - 1 - k)
                nc.vector.scalar_tensor_tensor(out=junk[0:BATCH, :], in0=c16[0:BATCH, H_LABEL:H_LABEL + ROWS],
                                               scalar=entry[:, k:k + 1], in1=block_map[:, k, :],
                                               op0=ALU.is_equal, op1=ALU.mult,
                                               accum_out=entry[:, k - 1:k]).then_inc(entries_ready, 1)
            dve.wait_ge(entry_psum, 1)
            link(nc.vector.scalar_tensor_tensor(out=junk32[:], in0=bank[6][:, 0:BLOCKS], scalar=1.0,
                                                in1=c32[:, C_DIAG:C_DIAG + BLOCKS], op0=ALU.mult, op1=ALU.mult,
                                                accum_out=entry0[:]))
            dve.wait_ge(exit_ready, 1)
            for r in range(BLOCK - 1, -1, -1):
                if r == BLOCK - 1:
                    link(nc.vector.tensor_scalar(within[:, r, :], half16(c16, H_TWICE), entry0[:, 0:1], None, ALU.is_lt))
                else:
                    link(nc.vector.tensor_scalar(within[:, r, :], half16(c16, H_TWICE2), q[:, r + 1:r + 2], None,
                                                 ALU.is_lt))
                link(nc.vector.tensor_tensor_reduce(out=junk[:], in0=within[:, r, :], in1=exit2[:, r, :], scale=1.0,
                                                    scalar=0.0, op0=ALU.mult, op1=ALU.max, accum_out=q[:, r:r + 1]))
                nc.vector.scalar_tensor_tensor(out=path[:, r, :], in0=half16(c16, H_TWICE4), scalar=q[:, r:r + 1],
                                               in1=within[:, r, :], op0=ALU.is_gt, op1=ALU.mult).then_inc(path_ready, 1)
            dve.wait_ge(gate_ready, 1)
            dve.wait_ge(attn_psum, 1)
            for n in range(TILES):
                nc.vector.scalar_tensor_tensor(out=x1[:, n, :], in0=bank[n][:, 0:DIM], scalar=tg[:, 0:1],
                                               in1=x[:, n, :], op0=ALU.mult, op1=ALU.add).then_inc(x1_ready, 1)
            dve.wait_ge(x1_ready, TILES)
            norm(x1, None, xn, var2_ready, std2_ready, xn2_ready)
            for h in range(HALVES):
                dve.wait_ge(xT_psum, h + 1)
                nc.vector.tensor_copy(xT[:, h * 512:(h + 1) * 512], bank[6 + h][:]).then_inc(xT_ready, 1)
                dve.wait_ge(xT_ready, h + 1)
                dve.wait_ge(xT_hi_ready, h + 1)
                nc.vector.tensor_tensor(out=xT_lo[:, h * 512:(h + 1) * 512], in0=xT[:, h * 512:(h + 1) * 512],
                                        in1=xT_hi[:, h * 512:(h + 1) * 512].bitcast(F32), op=ALU.subtract)\
                    .then_inc(xT_lo_ready, 1)

            def wide(a, n):
                return a.unsqueeze(2).to_broadcast([P, TILES, n])

            def router():
                top, total, inv, best, where, spare = tile1
                dve.wait_ge(router_psum, 1)
                link(nc.vector.tensor_copy(logit[:], bank[6][:, 0:64].rearrange("p (n e) -> p n e", n=TILES)))
                link(nc.vector.tensor_reduce(out=top[:], in_=logit[:], axis=AX.X, op=ALU.max))
                nc.vector.tensor_tensor(out=shifted[:], in0=logit[:], in1=wide(top[:], EXPERTS), op=ALU.subtract)\
                    .then_inc(shifted_ready, 1)
                mine = logit[:].unsqueeze(3).to_broadcast([P, TILES, EXPERTS, EXPERTS])
                others = logit[:].unsqueeze(2).to_broadcast([P, TILES, EXPERTS, EXPERTS])
                earlier = c32[:, C_EARLIER:C_EARLIER + 64].rearrange("p (e o) -> p e o", e=EXPERTS)
                link(nc.vector.tensor_tensor(out=pair[:], in0=others, in1=mine, op=ALU.is_equal))
                link(nc.vector.tensor_tensor(out=pair[:], in0=pair[:],
                                             in1=earlier.unsqueeze(1).to_broadcast([P, TILES, EXPERTS, EXPERTS]),
                                             op=ALU.mult))
                link(nc.vector.tensor_tensor(out=pair2[:], in0=others, in1=mine, op=ALU.is_gt))
                link(nc.vector.tensor_tensor(out=pair[:], in0=pair[:], in1=pair2[:], op=ALU.add))
                link(nc.vector.tensor_reduce(out=rank[:], in_=pair[:], axis=AX.X, op=ALU.add))
                dve.wait_ge(choice_psum, 1)
                link(nc.vector.tensor_scalar(choice[:], bank[7][:, 0:64].rearrange("p (n e) -> p n e", n=TILES)[:, :, 0:MAX_K],
                                             -30.0, 30.0, ALU.max, ALU.min))
                link(nc.vector.tensor_reduce(out=best[:], in_=choice[:], axis=AX.X, op=ALU.max))
                link(nc.vector.tensor_tensor(out=first[:], in0=choice[:], in1=wide(best[:], MAX_K), op=ALU.is_equal))
                order = c32[:, C_ORDER:C_ORDER + MAX_K].unsqueeze(1).to_broadcast([P, TILES, MAX_K])
                link(nc.vector.tensor_tensor(out=first[:], in0=first[:], in1=order, op=ALU.mult))
                link(nc.vector.tensor_reduce(out=where[:], in_=first[:], axis=AX.X, op=ALU.max))
                link(nc.vector.tensor_tensor(out=rank[:], in0=rank[:], in1=wide(where[:], EXPERTS), op=ALU.add))
                link(nc.vector.tensor_scalar(rank[:], rank[:], MAX_K + 1.0, tg[:, 1:2], ALU.is_lt, ALU.mult))
                dve.wait_ge(exp_ready, 1)
                link(nc.vector.tensor_reduce(out=total[:], in_=prob[:], axis=AX.X, op=ALU.add))
                link(nc.vector.reciprocal(inv[:], total[:]))
                link(nc.vector.tensor_tensor(out=prob[:], in0=prob[:], in1=wide(inv[:], EXPERTS), op=ALU.mult))
                link(nc.vector.tensor_tensor(out=score[:], in0=prob[:], in1=rank[:], op=ALU.mult))

            def product(v):
                dve.wait_ge(silu_ready, v + 1)
                if v >= 2:
                    dve.wait_ge(act_hi_ready, v - 1)
                    dve.wait_ge(act_lo_ready, v - 1)
                nc.vector.tensor_tensor(out=act[:, v % 2, :], in0=silu[:, v % 2, :], in1=bank[2 + v % 2][0:SUB, :],
                                        op=ALU.mult).then_inc(act_ready, 1)

            def low_part(v):
                dve.wait_ge(act_ready, v + 1)
                dve.wait_ge(act_hi_ready, v + 1)
                if v >= 2 * SUBS:
                    dve.wait_ge(down_psum, v // SUBS - 1)
                slot = v % (2 * SUBS)
                nc.vector.tensor_tensor(out=act_lo[:, slot, :], in0=act[:, v % 2, :],
                                        in1=act_hi[:, slot, :].bitcast(F32), op=ALU.subtract).then_inc(act_lo_ready, 1)

            def accumulate(u):
                h, e = units[u]
                dve.wait_ge(down_psum, u + 1)
                if e:
                    dve.wait_ge(acc_ready, BATCH * u)
                for b in range(BATCH):
                    n = h * BATCH + b
                    nc.vector.scalar_tensor_tensor(out=acc[:, n, :], in0=bank[4 + u % 2][:, b * DIM:(b + 1) * DIM],
                                                   scalar=score[:, n, e:e + 1], in1=(acc if e else x1)[:, n, :],
                                                   op0=ALU.mult, op1=ALU.add).then_inc(acc_ready, 1)

            total = len(units) * SUBS
            for v in range(total):
                product(v)
                if v:
                    low_part(v - 1)
                if v == 1:
                    router()
                if v >= 5 and v % SUBS == SUBS - 1:
                    accumulate(v // SUBS - 1)
            low_part(total - 1)
            accumulate(len(units) - 1)

        @block.tensor
        def _(pe):
            mm = nc.tensor.matmul
            pe.wait_ge(cleared, 2)
            pe.wait_ge(gates_in, 16)
            mm(bank[6][:, 0:2], ones[0:1, :], gin[:], start=True, stop=True).then_inc(gate_psum, 1)
            pe.wait_ge(c32_in, 16)
            for n in range(TILES):
                pe.wait_ge(xn_ready, n + 1)
                nc.tensor.transpose(bank[n // 4][:, (n % 4) * P:(n % 4 + 1) * P], xn[:, n, :], ident).then_inc(xnT_psum, 1)
            pe.wait_ge(ctxsq_ready, 1)
            pe.wait_ge(xnT_ready, 2)
            for n in range(TILES):
                b = n % BATCH
                dst = bank[2 + n // 2][:, (n % 2) * ROWS:(n % 2 + 1) * ROWS]
                mm(dst, xnT[:, n * P:(n + 1) * P], ctxT[:, b * ROWS:(b + 1) * ROWS], start=True, stop=False)
                mm(dst, ones[:], ctxsq[:, b * ROWS:(b + 1) * ROWS], start=False, stop=True).then_inc(dot_psum, 1)
            pe.wait_ge(c16_in, 16)
            pe.wait_ge(masks_moved, 16 * 2 * HALVES * len(CHUNK_ENDS))
            pe.wait_ge(sqdist_ready, TILES)
            pe.wait_ge(xnT_ready, 2)
            for r in range(BLOCK):
                for plane in range(2):
                    for h in range(HALVES):
                        at = (r % 2) * ROWS + h * P
                        src = KT[:, h, plane].rearrange("p b (k r) -> p (b k) r", r=BLOCK)[:, :, r]
                        last = nc.tensor.transpose(bank[plane * 4 + r // 2][:].bitcast(F16)[:, at:at + P], src, ident16)
                last.then_inc(masks_psum, 1)
            pe.wait_ge(entries_ready, BLOCKS - 1)
            pe.wait_ge(gate_ready, 1)
            mm(bank[6][:, 0:BLOCKS], c32[0:BATCH, C_BATCH:C_BATCH + P], entry[:], start=True, stop=True)\
                .then_inc(entry_psum, 1)
            pe.wait_ge(ctxb_in, 16)
            pe.wait_ge(up_ready, BLOCK // 2)
            pe.wait_ge(notleft_ready, BLOCK // 2)
            for i, r in enumerate(range(BLOCK - 1, -1, -1)):
                pe.wait_ge(path_ready, i + 1)
                for h in range(HALVES):
                    for b in range(BATCH):
                        last = mm(bank[h * BATCH + b][:, 0:DIM], path[b * QUAD:(b + 1) * QUAD, r, h * P:(h + 1) * P],
                                  ctxb[b * QUAD:(b + 1) * QUAD, r, :], start=(i == 0), stop=(i == BLOCK - 1))
            last.then_inc(attn_psum, 1)
            for n in range(TILES):
                pe.wait_ge(xn2_ready, n + 1)
                last = nc.tensor.transpose(bank[6 + n // 4][:, (n % 4) * P:(n % 4 + 1) * P], xn[:, n, :], ident)
                if n % 4 == 3:
                    last.then_inc(xT_psum, 1)

            def split_mm(dst, w_hi, w_lo, a_hi, a_lo, start, stop):
                mm(dst, w_hi, a_hi, start=start, stop=False)
                mm(dst, w_hi, a_lo, start=False, stop=False)
                return mm(dst, w_lo, a_hi, start=False, stop=stop)

            def gate_up(v):
                h, e = units[v // SUBS]
                m = v % SUBS
                if v % (SUBS * EXPERTS) == 0:
                    pe.wait_ge(xT_lo_ready, h + 1)
                    pe.wait_ge(xT_hi_ready, h + 1)
                if v >= 2:
                    pe.wait_ge(act_ready, v - 1)
                tok = slice(h * 512, (h + 1) * 512)
                for part in range(2):
                    col = slice(m * SUB, (m + 1) * SUB)
                    last = split_mm(bank[2 * part + v % 2][0:SUB, :], gu_hi[:, e, part, col], gu_lo[:, e, part, col],
                                    xT_hi[:, tok], xT_lo[:, tok], True, True)
                last.then_inc(gu_psum, 1)

            def down(u):
                h, e = units[u]
                pe.wait_ge(act_hi_ready, SUBS * (u + 1))
                pe.wait_ge(act_lo_ready, SUBS * (u + 1))
                if u >= 2:
                    pe.wait_ge(acc_ready, BATCH * (u - 1))
                for b in range(BATCH):
                    for m in range(SUBS):
                        slot = (u * SUBS + m) % (2 * SUBS)
                        tok, col = slice(b * P, (b + 1) * P), slice(m * DIM, (m + 1) * DIM)
                        last = split_mm(bank[4 + u % 2][:, b * DIM:(b + 1) * DIM], act_hi[:, slot, tok],
                                        act_lo[:, slot, tok], dn_hi[:, e, col], dn_lo[:, e, col],
                                        m == 0, m == SUBS - 1)
                last.then_inc(down_psum, 1)

            pe.wait_ge(w_lo_ready, 2 * EXPERTS)
            for u in range(len(units)):
                for m in range(SUBS):
                    gate_up(u * SUBS + m)
                    if u and m == 1:
                        down(u - 1)
                    if u == 0 and m == 1:
                        pe.wait_ge(router_in, 80)
                        pe.wait_ge(xT_ready, HALVES)
                        pe.wait_ge(xT_hi_ready, HALVES)
                        for n in range(TILES):
                            last = mm(bank[6][:, n * EXPERTS:(n + 1) * EXPERTS], xT[:, n * P:(n + 1) * P], wr[:],
                                      start=True, stop=True)
                        last.then_inc(router_psum, 1)
                        for h in range(HALVES):
                            if h:
                                pe.wait_ge(actor_ready, h)
                            mm(bank[7][0:ACTOR, :], wa1[:], xT[:, h * 512:(h + 1) * 512], start=True, stop=True)\
                                .then_inc(actor_psum, 1)
                        pe.wait_ge(actor_ready, HALVES)
                        for n in range(TILES):
                            dst = bank[7][:, n * EXPERTS:n * EXPERTS + MAX_K]
                            mm(dst, actor[:, n * P:(n + 1) * P], wa2[:], start=True, stop=False)
                            last = mm(dst, ones[0:1, :], ba2[:], start=False, stop=True)
                        last.then_inc(choice_psum, 1)
            down(len(units) - 1)


def constants():
    import numpy as np

    c32 = np.zeros((P, C_WIDTH), np.float32)
    p = np.arange(P)
    c32[p, C_IDENT + p] = 1
    c32[p, C_DIAG + p % BLOCKS] = 1
    c32[p // BLOCKS, C_BATCH + p] = 1
    e = np.arange(EXPERTS)
    c32[:, C_EARLIER:C_EARLIER + 64] = (e[None, :] < e[:, None]).reshape(-1)
    c32[:, C_ORDER:C_ORDER + MAX_K] = MAX_K - np.arange(MAX_K)
    c32[:, C_FIRST] = np.where(p % QUAD == 0, 0.0, FAR)
    c16 = np.zeros((P, H_WIDTH), np.float16)
    c16[p, H_IDENT + p] = 1
    j = np.arange(ROWS)
    for at, v in ((H_LABEL, 2 * j + 1), (H_TWICE, 2 * j), (H_TWICE2, 2 * j + 2), (H_TWICE4, 2 * j + 4)):
        c16[:, at:at + ROWS] = v * LABEL
    return c32, c16


def kernel(x, ctx_1024, g_xattn, g_ffn, L0_ffn_router_w, L0_ffn_actor_w1, L0_ffn_actor_b1, L0_ffn_actor_w2,
           L0_ffn_actor_b2, L0_ffn_gate_w, L0_ffn_up_w, L0_ffn_down_w):
    import numpy as np
    import concourse.bacc as bacc
    from concourse.bass_utils import run_bass_kernel_spmd

    a = np.asarray
    c32, c16 = constants()
    arrays = {
        "x_tok": a(x).reshape(BATCH, HALVES, P, DIM).transpose(2, 1, 0, 3).reshape(P, TILES, DIM),
        "ctx_t": a(ctx_1024).reshape(BATCH * ROWS, DIM).T,
        "ctx_blk": a(ctx_1024).reshape(BATCH * BLOCKS, BLOCK, DIM),
        "gates": np.concatenate([a(g_xattn), a(g_ffn)]).reshape(1, 2),
        "w_gate": a(L0_ffn_gate_w).transpose(2, 0, 1),
        "w_up": a(L0_ffn_up_w).transpose(2, 0, 1),
        "w_down": a(L0_ffn_down_w).reshape(EXPERTS, DIM, SUBS, SUB).transpose(3, 0, 2, 1).reshape(SUB, EXPERTS, SUBS * DIM),
        "w_router": a(L0_ffn_router_w).T,
        "w_a1": a(L0_ffn_actor_w1).T,
        "b_a1": a(L0_ffn_actor_b1).reshape(ACTOR, 1),
        "w_a2": a(L0_ffn_actor_w2).T,
        "b_a2": a(L0_ffn_actor_b2).reshape(1, MAX_K),
        "const32": c32,
        "const16": c16,
    }
    arrays = {k: np.ascontiguousarray(v) for k, v in arrays.items()}
    nc = bacc.Bacc("TRN2", target_bir_lowering=False, num_devices=1)
    aps = [nc.dram_tensor(k, v.shape, mybir.dt.from_np(v.dtype), kind="ExternalInput").ap() for k, v in arrays.items()]
    out = nc.dram_tensor("out", (P, HALVES, BATCH, DIM), mybir.dt.float32, kind="ExternalOutput").ap()
    dist_dram = nc.dram_tensor("dist_dram", (BATCH * ROWS, D_WIDTH), mybir.dt.float32, kind="Internal").ap()
    mask_dram = nc.dram_tensor("mask_dram", (BATCH, ROWS, 2, M_WIDTH), mybir.dt.float16, kind="Internal").ap()
    build(nc, *aps, dist_dram, mask_dram, out)
    r = run_bass_kernel_spmd(nc, [arrays], core_ids=[0])
    got = a(r.results[0]["out"])
    return got.transpose(2, 1, 0, 3).reshape(BATCH, ROWS, DIM)
```

```python
from contextlib import ExitStack

import concourse.bass as bass
from concourse import mybir

BATCH, ROWS, DIM = 4, 256, 128
EXPERTS, INNER, MAX_K, ACTOR = 8, 336, 6, 50
P = 128
TILES = BATCH * ROWS // P
HALVES = ROWS // P
LANE_COLS = 16
LANES = ROWS // LANE_COLS
QUAD = 32
LAG = 2
GROUP = 8
RING = 4 * GROUP
STEPS = 288
GROUPS = STEPS // GROUP
TURNS = STEPS // RING
BLOCK = 8
BLOCKS = ROWS // BLOCK
CHUNK_ENDS = [96, 192, 240, 256]
SKEW = LAG * (LANES - 1)
D_WIDTH = ROWS + 2 * SKEW + 4
M_PAD = 32
M_WIDTH = STEPS + M_PAD + 8
SUB = 112
SUBS = INNER // SUB
HALF_TOKENS = BATCH * P
FAR = 1e30
LABEL = 1.0 / 1024

UNITS = HALVES * EXPERTS
V_TOTAL = UNITS * SUBS
V_SCORES = 4


def v_wide(u):
    return max(SUBS * u + 3, V_SCORES + 1)


def v_scale(u):
    return SUBS * u + 6


def v_turn(h):
    return v_scale((h + 1) * EXPERTS - 1) + (2 if h < HALVES - 1 else 0)


def adds(u):
    return u - u // EXPERTS

C_IDENT, C_DIAG, C_BATCH, C_EARLIER, C_ORDER, C_FIRST, C_MINE, C_PICK = 0, 128, 160, 288, 352, 360, 361, 365
C_WIDTH = 373
H_IDENT, H_LABEL, H_TWICE, H_TWICE2, H_TWICE4 = 0, 128, 384, 640, 896
H_WIDTH = 1152


def build(nc, x_tok, ctx_t, ctx_blk, gates, w_gate, w_up, w_down, w_router, w_a1, b_a1, w_a2, b_a2,
          const32, const16, dist_dram, mask_dram, out):
    F32, F16, F32R = mybir.dt.float32, mybir.dt.float16, mybir.dt.float32r
    ALU, ACT, AX = mybir.AluOpType, mybir.ActivationFunctionType, mybir.AxisListType

    with ExitStack() as stack:
        def sb(name, shape, dtype=F32):
            return stack.enter_context(nc.sbuf_tensor(name, shape, dtype))

        def sem(name):
            return stack.enter_context(nc.semaphore(name))

        x = sb("x", [P, TILES, DIM])
        c32 = sb("c32", [P, C_WIDTH])
        c16 = sb("c16", [P, H_WIDTH], F16)
        ones = sb("ones", [P, P])
        gin = sb("gin", [1, 2])
        tg = sb("tg", [P, 2])
        stats = sb("stats", [P, TILES, 6])
        mv = sb("mv", [P, TILES, 2])
        var = sb("var", [P, TILES])
        std = sb("std", [P, TILES])
        rstd = sb("rstd", [P, TILES])
        xn = sb("xn", [P, TILES, DIM])
        bb = sb("bb", [P, TILES])
        entry = sb("entry", [BATCH, BLOCKS])
        gu_hi = sb("gu_hi", [P, EXPERTS, 2, INNER], F32R)
        dn_hi = sb("dn_hi", [SUB, EXPERTS, SUBS * DIM], F32R)
        with nc.sbuf_tensor("gu_w", [P, EXPERTS, 2, INNER], F32) as gu_w, \
                nc.sbuf_tensor("dn_w", [SUB, EXPERTS, SUBS * DIM], F32) as dn_w:
            pass
        gu_lo = sb("gu_lo", [P, EXPERTS, 2, INNER], F32R)
        dn_lo = sb("dn_lo", [SUB, EXPERTS, SUBS * DIM], F32R)
        wr = sb("wr", [P, EXPERTS])
        wa1 = sb("wa1", [P, ACTOR])
        ba1 = sb("ba1", [ACTOR, 1])
        wa2 = sb("wa2", [ACTOR, MAX_K])
        ba2 = sb("ba2", [1, MAX_K])

        pick = sb("pick", [2 * EXPERTS, EXPERTS, P], F32R)

        alignment = ExitStack()

        def sb(name, shape, dtype=F32):
            return alignment.enter_context(nc.sbuf_tensor(name, shape, dtype))

        KT = sb("KT", [P, HALVES, 2, BATCH, ROWS], F16)
        ctxb = sb("ctxb", [P, BLOCK, DIM])
        ctx_part = sb("ctx_part", [P, BLOCK, DIM], F32R)
        ctx_hi = sb("ctx_hi", [P, BLOCK, BATCH, DIM], F32R)
        ctx_lo = sb("ctx_lo", [P, BLOCK, BATCH, DIM], F32R)

        early = ExitStack()

        def sb(name, shape, dtype=F32):
            return early.enter_context(nc.sbuf_tensor(name, shape, dtype))

        ctxT = sb("ctxT", [P, BATCH * ROWS])
        ctxsq = sb("ctxsq", [P, BATCH * ROWS])
        sq_junk = sb("sq_junk", [P, DIM])
        xnT = sb("xnT", [P, TILES * P])
        DT = sb("DT", [P, TILES, D_WIDTH])
        Dk = sb("Dk", [P, LANE_COLS, STEPS])
        Dring = sb("Dring", [P, RING, LANE_COLS])
        ring = sb("ring", [P, RING, LANE_COLS + 1])
        mring = sb("mring", [P, RING, LANE_COLS])
        diff = sb("diff", [P, 2, 2, GROUP, LANE_COLS])
        K = sb("K", [P, LANE_COLS, 2, STEPS + 2], F16)
        early.close()

        def sb(name, shape, dtype=F32):
            return alignment.enter_context(nc.sbuf_tensor(name, shape, dtype))

        notleft = sb("notleft", [P, BLOCK, ROWS], F16)
        up = sb("up", [P, BLOCK, ROWS], F16)
        exit2 = sb("exit2", [P, BLOCK, ROWS], F16)
        upsum = sb("upsum", [P, BLOCK, ROWS], F16)
        lab = sb("lab", [P, 2, ROWS + 1], F16)
        lab_t = sb("lab_t", [P, ROWS], F16)
        lab_e = sb("lab_e", [P, ROWS], F16)
        block_map = sb("block_map", [BATCH, BLOCKS, ROWS], F16)
        junk = sb("junk", [P, ROWS])
        entry0 = sb("entry0", [P, 1])
        junk32 = sb("junk32", [P, BLOCKS])
        within = sb("within", [P, BLOCK, ROWS], F16)
        q = sb("q", [P, BLOCK])
        path = sb("path", [P, BLOCK, ROWS], F32R)
        alignment.close()

        def sb(name, shape, dtype=F32):
            return stack.enter_context(nc.sbuf_tensor(name, shape, dtype))

        x1 = sb("x1", [P, TILES, DIM])
        xT = sb("xT", [P, TILES * P])
        xT_hi = sb("xT_hi", [P, TILES * P], F32R)
        xT_lo = sb("xT_lo", [P, TILES * P], F32R)
        actor = sb("actor", [ACTOR, TILES * P])
        logit = sb("logit", [P, TILES, EXPERTS])
        shifted = sb("shifted", [P, TILES, EXPERTS])
        prob = sb("prob", [P, TILES, EXPERTS])
        tile1 = [sb(f"tile1_{i}", [P, TILES]) for i in range(6)]
        pair = sb("pair", [P, TILES, EXPERTS, EXPERTS])
        pair2 = sb("pair2", [P, TILES, EXPERTS, EXPERTS])
        rank = sb("rank", [P, TILES, EXPERTS])
        choice = sb("choice", [P, TILES, MAX_K])
        first = sb("first", [P, TILES, MAX_K])
        silu = sb("silu", [SUB, 2, HALF_TOKENS])
        act = sb("act", [SUB, 2, HALF_TOKENS])
        act_hi = sb("act_hi", [SUB, 2 * SUBS, HALF_TOKENS], F32R)
        act_lo = sb("act_lo", [SUB, 2 * SUBS, HALF_TOKENS], F32R)
        score_r = sb("score_r", [P, TILES, EXPERTS], F32R)
        score2 = sb("score2", [P, TILES, 2 * EXPERTS])
        scoreT = sb("scoreT", [2 * EXPERTS, TILES * P], F32R)
        score_wide = sb("score_wide", [P, 2, HALF_TOKENS])
        scaled = sb("scaled", [P, 2, HALF_TOKENS])
        acc = sb("acc", [P, HALVES, HALF_TOKENS])
        result = sb("result", [P, TILES, DIM])
        bank = [stack.enter_context(nc.psum_tensor(f"bank{i}", [P, 512], F32)) for i in range(8)]

        x_in, ctx_in, c32_in, c16_in, ctxb_in = map(sem, ("x_in", "ctx_in", "c32_in", "c16_in", "ctxb_in"))
        gates_in, weights_in, router_in = map(sem, ("gates_in", "weights_in", "router_in"))
        cleared = sem("cleared")
        ring_clear = sem("ring_clear")
        dve_step = sem("dve_step")
        var_ready, std_ready, xn_ready = map(sem, ("var_ready", "std_ready", "xn_ready"))
        bb_ready, xnT_psum, xnT_ready, ctxsq_ready = map(sem, ("bb_ready", "xnT_psum", "xnT_ready", "ctxsq_ready"))
        gate_psum, gate_ready = map(sem, ("gate_psum", "gate_ready"))
        dot_psum, sqdist_ready, dist_ready = map(sem, ("dot_psum", "sqdist_ready", "dist_ready"))
        dist_stored, lanes_in = sem("dist_stored"), sem("lanes_in")
        masks_stored = sem("masks_stored")
        dring_ready = sem("dring_ready")
        sweep = sem("sweep")
        diff_ready = sem("diff_ready")
        signs_ready = sem("signs_ready")
        masks_moved = sem("masks_moved")
        w_hi_ready, w_lo_ready = sem("w_hi_ready"), sem("w_lo_ready")
        masks_psum, notleft_ready, up_ready, exit_ready = map(sem, ("masks_psum", "notleft_ready", "up_ready", "exit_ready"))
        up_label_ready, upsum_ready = sem("up_label_ready"), sem("upsum_ready")
        labels_ready, map_moved, entries_ready = map(sem, ("labels_ready", "map_moved", "entries_ready"))
        entry_psum, path_ready, attn_psum, x1_ready = map(sem, ("entry_psum", "path_ready", "attn_psum", "x1_ready"))
        var2_ready, std2_ready, xn2_ready = map(sem, ("var2_ready", "std2_ready", "xn2_ready"))
        xT_psum, xT_ready, xT_hi_ready, xT_lo_ready = map(sem, ("xT_psum", "xT_ready", "xT_hi_ready", "xT_lo_ready"))
        router_psum, actor_psum, actor_ready, choice_psum = map(sem, ("router_psum", "actor_psum", "actor_ready", "choice_psum"))
        shifted_ready, exp_ready = sem("shifted_ready"), sem("exp_ready")
        gu_psum, silu_ready, act_ready, act_hi_ready, act_lo_ready = map(
            sem, ("gu_psum", "silu_ready", "act_ready", "act_hi_ready", "act_lo_ready"))
        down_psum, scaled_ready, acc_ready, out_done = map(sem, ("down_psum", "scaled_ready", "acc_ready", "out_done"))
        ctx_hi_ready, ctx_low, ctx_lo_ready = map(sem, ("ctx_hi_ready", "ctx_low", "ctx_lo_ready"))
        pick_ready, score_ready, scoreT_psum, scoreT_ready = map(
            sem, ("pick_ready", "score_ready", "scoreT_psum", "scoreT_ready"))
        wide_psum, wide_ready = sem("wide_psum"), sem("wide_ready")
        acc_psum, result_ready = sem("acc_psum"), sem("result_ready")
        stack.enter_context(nc.allow_non_contiguous_dma(reason="single columns of small operands"))
        block = stack.enter_context(nc.Block())

        ident = c32[:, C_IDENT:C_IDENT + P]
        ident16 = c16[:, H_IDENT:H_IDENT + P]

        def half16(t, at):
            return t[:, at:at + ROWS]

        units = [(h, e) for h in range(HALVES) for e in range(EXPERTS)]

        @block.sync
        def _(sp):
            sp.dma_start(x[:], x_tok).then_inc(x_in, 16)
            sp.dma_start(c32[:], const32).then_inc(c32_in, 16)
            sp.dma_start(gin[:], gates).then_inc(gates_in, 16)
            for h in range(HALVES):
                sp.wait_ge(dist_ready, BATCH * (h + 1))
                sp.dma_start(bass.AP(dist_dram.tensor, h * P * D_WIDTH,
                                     [[D_WIDTH, P], [ROWS * D_WIDTH, BATCH], [1, D_WIDTH]]),
                             DT[:, h * BATCH:(h + 1) * BATCH, :]).then_inc(dist_stored, 16)
            sp.wait_ge(dist_stored, 16 * HALVES)
            sp.wait_ge(cleared, 1)
            for b in range(BATCH):
                src = bass.AP(dist_dram.tensor, b * ROWS * D_WIDTH + SKEW,
                              [[LANE_COLS * D_WIDTH - LAG, LANES], [D_WIDTH, LANE_COLS], [1, STEPS]])
                sp.dma_start(Dk[b * QUAD:b * QUAD + LANES, :, :], src).then_inc(lanes_in, 16)
            begin, sent = 0, 0
            for chunk, end in enumerate(CHUNK_ENDS):
                groups = -(-(end + SKEW) // GROUP)
                upto = groups * GROUP + 1
                sp.wait_ge(signs_ready, 2 * groups)
                for b in range(BATCH):
                    dst = bass.AP(mask_dram.tensor, b * 2 * ROWS * M_WIDTH + sent + M_PAD - 1,
                                  [[2 * LANE_COLS * M_WIDTH - LAG, LANES], [M_WIDTH, 2 * LANE_COLS],
                                   [1, upto - sent]])
                    sp.dma_start(dst, K[b * QUAD:b * QUAD + LANES, :, :, sent:upto]
                                 .rearrange("c j m t -> c (j m) t")).then_inc(masks_stored, 16)
                sp.wait_ge(masks_stored, 16 * BATCH * (chunk + 1))
                for h in range(HALVES):
                    for plane in range(2):
                        src = bass.AP(mask_dram.tensor, (h * P * 2 + plane) * M_WIDTH + M_PAD + begin,
                                      [[2 * M_WIDTH, P], [2 * ROWS * M_WIDTH, BATCH], [1, end - begin]])
                        sp.dma_start(KT[:, h, plane, :, begin:end], src).then_inc(masks_moved, 16)
                begin, sent = end, upto
            sp.wait_ge(labels_ready, 1)
            for b in range(BATCH):
                sp.dma_start(block_map[b:b + 1, :, :], lab[b * BLOCKS:(b + 1) * BLOCKS, 0, 1:ROWS + 1])\
                  .then_inc(map_moved, 16)
            for h in range(HALVES):
                sp.wait_ge(result_ready, h + 1)
                sp.dma_start(out[:, h], result[:, h * BATCH:(h + 1) * BATCH, :]).then_inc(out_done, 16)
            sp.wait_ge(out_done, 16 * HALVES)

        @block.gpsimd
        def _(pool):
            nc.gpsimd.memset(Dk[:], FAR).then_inc(cleared, 1)
            nc.gpsimd.memset(ones[:], 1.0).then_inc(cleared, 1)
            nc.gpsimd.memset(K[:, :, :, 0:2], 0.0).then_inc(cleared, 1)

            def group_diffs(q_, group, head):
                s = q_ * GROUP
                pool.wait_ge(sweep, 3 * GROUP * (group + 1))
                if not head or q_ >= 2:
                    pool.wait_ge(signs_ready, group * 2 - 2)
                left = ring[:, s:s + GROUP, 0:LANE_COLS]
                nc.gpsimd.tensor_tensor(out=diff[:, q_ % 2, 0], in0=left, in1=mring[:, s:s + GROUP, :],
                                        op=ALU.subtract).then_inc(diff_ready, 1)
                nc.gpsimd.tensor_tensor(out=diff[:, q_ % 2, 1], in0=left, in1=ring[:, s:s + GROUP, 1:LANE_COLS + 1],
                                        op=ALU.subtract).then_inc(diff_ready, 1)

            for q_ in range(4):
                group_diffs(q_, q_, True)
            pool.wait_ge(ctx_hi_ready, 1)
            nc.gpsimd.tensor_tensor(out=ctxb[:], in0=ctxb[:], in1=ctx_part[:].bitcast(F32), op=ALU.subtract)\
                .then_inc(ctx_low, 1)
            with pool.Fori(1, TURNS) as k:
                for q_ in range(4):
                    group_diffs(q_, k * 4 + q_, False)
                pool.wait_ge(w_hi_ready, k * 2)
                nc.gpsimd.tensor_tensor(out=gu_lo[:, bass.ds(k - 1, 1)], in0=gu_w[:, bass.ds(k - 1, 1)],
                                        in1=gu_hi[:, bass.ds(k - 1, 1)].bitcast(F32), op=ALU.subtract)\
                    .then_inc(w_lo_ready, 1)
                nc.gpsimd.tensor_tensor(out=dn_lo[:, bass.ds(k - 1, 1)], in0=dn_w[:, bass.ds(k - 1, 1)],
                                        in1=dn_hi[:, bass.ds(k - 1, 1)].bitcast(F32), op=ALU.subtract)\
                    .then_inc(w_lo_ready, 1)
            pool.wait_ge(up_label_ready, 1)
            pool.wait_ge(c16_in, 16)
            nc.gpsimd.tensor_tensor(out=upsum[:], in0=upsum[:],
                                    in1=half16(c16, H_TWICE2).unsqueeze(1).to_broadcast([P, BLOCK, ROWS]),
                                    op=ALU.add).then_inc(upsum_ready, 1)
            pool.wait_ge(upsum_ready, 1)
            pool.wait_ge(notleft_ready, BLOCK // 2)
            nc.gpsimd.tensor_tensor(out=exit2[:], in0=upsum[:], in1=notleft[:], op=ALU.mult).then_inc(exit_ready, 1)
            for u in range(UNITS):
                h, e = units[u]
                if 0 < e < EXPERTS - 1:
                    pool.wait_ge(scaled_ready, u + 1)
                    if e > 1:
                        pool.wait_ge(acc_ready, adds(u) - 1)
                    nc.gpsimd.tensor_tensor(out=acc[:, h], in0=acc[:, h], in1=scaled[:, u % 2], op=ALU.add)\
                        .then_inc(acc_ready, 1)

        @block.scalar
        def _(sc):
            sc.dma_start(ctxT[:], ctx_t).then_inc(ctx_in, 16)
            sc.dma_start(c16[:], const16).then_inc(c16_in, 16)
            sc.dma_start(ctxb[:], ctx_blk).then_inc(ctxb_in, 16)
            sc.dma_start(gu_w[:, :, 0, :], w_gate).then_inc(weights_in, 16)
            sc.dma_start(gu_w[:, :, 1, :], w_up).then_inc(weights_in, 16)
            sc.dma_start(dn_w[:], w_down).then_inc(weights_in, 16)
            for dst, src in ((wr, w_router), (wa1, w_a1), (ba1, b_a1), (wa2, w_a2), (ba2, b_a2)):
                sc.dma_start(dst[:], src).then_inc(router_in, 16)
            sc.wait_ge(gate_psum, 1)
            nc.scalar.activation(tg[:], bank[6][:, 0:2], ACT.Tanh).then_inc(gate_ready, 1)
            sc.wait_ge(var_ready, 1)
            nc.scalar.activation(std[:], var[:], ACT.Sqrt).then_inc(std_ready, 1)
            for n in range(TILES):
                sc.wait_ge(xn_ready, n + 1)
                if n:
                    sc.wait_ge(bb_ready, n)
                nc.scalar.activation(sq_junk[:], xn[:, n, :], ACT.Square, accum_out=bb[:, n:n + 1]).then_inc(bb_ready, 1)
            sc.wait_ge(xnT_psum, TILES)
            nc.scalar.activation(xnT[:, 512:1024], bank[1][:], ACT.Copy).then_inc(xnT_ready, 1)
            for n in range(TILES):
                sc.wait_ge(sqdist_ready, n + 1)
                nc.scalar.activation(DT[:, n, SKEW:SKEW + ROWS], DT[:, n, SKEW:SKEW + ROWS], ACT.Sqrt).then_inc(dist_ready, 1)

            def dist_group(slot, group_start):
                nc.scalar.activation(Dring[:, slot * GROUP:(slot + 1) * GROUP, :].rearrange("p t j -> p j t"),
                                     Dk[:, :, group_start], ACT.Copy).then_inc(dring_ready, 1)

            def sign_group(half, own, after):
                for plane, cols in ((0, own), (1, after)):
                    nc.scalar.activation(K[:, :, plane, cols], diff[:, half, plane].rearrange("p t j -> p j t"), ACT.Sign)\
                        .then_inc(signs_ready, 1)

            sc.wait_ge(lanes_in, 16 * BATCH)
            for g in range(4):
                dist_group(g, slice(g * GROUP, (g + 1) * GROUP))
            sc.wait_ge(ctxb_in, 16)
            sc.wait_ge(c32_in, 16)
            nc.scalar.activation(ctx_part[:], ctxb[:], ACT.Copy).then_inc(ctx_hi_ready, 1)
            sc.wait_ge(ctx_hi_ready, 1)
            for b in range(BATCH):
                nc.scalar.activation(ctx_hi[:, :, b, :], ctx_part[:].bitcast(F32), ACT.Copy,
                                     scale=c32[:, C_MINE + b:C_MINE + b + 1]).then_inc(ctx_hi_ready, 1)
            nc.scalar.activation(pick[:], c32[0:2 * EXPERTS, C_PICK:C_PICK + EXPERTS].unsqueeze(2)
                                 .to_broadcast([2 * EXPERTS, EXPERTS, P]), ACT.Copy).then_inc(pick_ready, 1)
            sc.wait_ge(weights_in, 48)
            sc.wait_ge(cleared, 3)
            with sc.Fori(0, TURNS - 1) as k:
                for s in range(4):
                    sc.wait_ge(sweep, k * (12 * GROUP) + 3 * GROUP * (s + 1))
                    dist_group(s, bass.ds(k * RING + (RING + s * GROUP), GROUP))
                    sc.wait_ge(diff_ready, k * 8 + 2 * (s + 1))
                    sign_group(s % 2, bass.ds(k * RING + (s * GROUP + 1), GROUP), bass.ds(k * RING + (s * GROUP + 2), GROUP))
                nc.scalar.activation(gu_hi[:, bass.ds(k, 1)], gu_w[:, bass.ds(k, 1)], ACT.Copy).then_inc(w_hi_ready, 1)
                nc.scalar.activation(dn_hi[:, bass.ds(k, 1)], dn_w[:, bass.ds(k, 1)], ACT.Copy).then_inc(w_hi_ready, 1)
            sc.wait_ge(ctx_low, 1)
            for b in range(BATCH):
                nc.scalar.activation(ctx_lo[:, :, b, :], ctxb[:], ACT.Copy,
                                     scale=c32[:, C_MINE + b:C_MINE + b + 1]).then_inc(ctx_lo_ready, 1)
            for g in range(GROUPS - 4, GROUPS):
                sc.wait_ge(diff_ready, 2 * (g + 1))
                sign_group(g % 2, slice(g * GROUP + 1, (g + 1) * GROUP + 1), slice(g * GROUP + 2, (g + 1) * GROUP + 2))
            for pr in range(BLOCK // 2):
                sc.wait_ge(masks_psum, 2 * (pr + 1))
                src = bank[4 + pr][:].bitcast(F16)[:, 0:2 * ROWS].rearrange("p (r j) -> p r j", r=2)
                nc.scalar.activation(up[:, 2 * pr:2 * pr + 2, :], src, ACT.Relu).then_inc(up_ready, 1)
            sc.wait_ge(up_ready, BLOCK // 2)
            nc.scalar.activation(upsum[:], up[:], ACT.Copy, scale=LABEL).then_inc(up_label_ready, 1)
            sc.wait_ge(var2_ready, 1)
            nc.scalar.activation(std[:], var[:], ACT.Sqrt).then_inc(std2_ready, 1)
            for h in range(HALVES):
                sc.wait_ge(xT_ready, h + 1)
                nc.scalar.activation(xT_hi[:, h * 512:(h + 1) * 512], xT[:, h * 512:(h + 1) * 512], ACT.Copy).then_inc(xT_hi_ready, 1)

            def silu_tile(v):
                sc.wait_ge(gu_psum, v + 1)
                if v >= 2:
                    sc.wait_ge(act_ready, v - 1)
                nc.scalar.activation(silu[:, v % 2, :], bank[v % 2][0:SUB, :], ACT.Silu).then_inc(silu_ready, 1)

            def high_part(v):
                sc.wait_ge(act_ready, v + 1)
                if v >= 2 * SUBS:
                    sc.wait_ge(down_psum, v - 2 * SUBS + 1)
                nc.scalar.activation(act_hi[:, v % (2 * SUBS), :], act[:, v % 2, :], ACT.Copy).then_inc(act_hi_ready, 1)

            for v in range(v_wide(UNITS - 1) + 2):
                if 1 <= v <= V_TOTAL:
                    high_part(v - 1)
                if v == V_SCORES + 1:
                    for h in range(HALVES):
                        sc.wait_ge(scoreT_psum, h + 1)
                        nc.scalar.activation(scoreT[:, h * 512:(h + 1) * 512], bank[6 + h][0:2 * EXPERTS, :], ACT.Copy)\
                            .then_inc(scoreT_ready, 1)
                for u in range(UNITS):
                    if v == v_wide(u) + 1:
                        sc.wait_ge(wide_psum, u + 1)
                        if u >= 2:
                            sc.wait_ge(scaled_ready, u - 1)
                        nc.scalar.activation(score_wide[:, u % 2], bank[6][:], ACT.Copy).then_inc(wide_ready, 1)
                if v < V_TOTAL:
                    silu_tile(v)
                if v == 1:
                    for h in range(HALVES):
                        sc.wait_ge(actor_psum, h + 1)
                        sc.wait_ge(router_in, 80)
                        nc.scalar.activation(actor[:, h * 512:(h + 1) * 512], bank[4 + h][0:ACTOR, :], ACT.Gelu_apprx_tanh,
                                             bias=ba1[:, 0:1]).then_inc(actor_ready, 1)
                    sc.wait_ge(shifted_ready, 1)
                    nc.scalar.activation(prob[:], shifted[:], ACT.Exp).then_inc(exp_ready, 1)

        @block.vector
        def _(dve):
            steps = [0]

            def link(ins):
                steps[0] += 1
                ins.then_inc(dve_step, 1)
                dve.wait_ge(dve_step, steps[0])

            def norm(src, own, dst, var_sem, std_sem, out_sem):
                for n in range(TILES):
                    nc.vector.bn_stats(stats[:, n, :], src[:, n, :]).then_inc(dve_step, 1)
                steps[0] += TILES
                dve.wait_ge(dve_step, steps[0])
                for n in range(TILES):
                    nc.vector.bn_aggr(mv[:, n, :], stats[:, n, :]).then_inc(dve_step, 1)
                steps[0] += TILES
                dve.wait_ge(dve_step, steps[0])
                nc.vector.tensor_scalar(var[:], mv[:, :, 1], 1e-5, None, ALU.add).then_inc(var_sem, 1)
                dve.wait_ge(std_sem, 1)
                link(nc.vector.reciprocal(rstd[:], std[:]))
                for n in range(TILES):
                    nc.vector.tensor_scalar(dst[:, n, :], src[:, n, :], mv[:, n, 0:1], rstd[:, n:n + 1],
                                            ALU.subtract, ALU.mult).then_inc(out_sem, 1)

            nc.vector.memset(ring[:], FAR).then_inc(ring_clear, 1)
            nc.vector.memset(DT[:], FAR).then_inc(ring_clear, 1)
            dve.wait_ge(x_in, 16)
            norm(x, None, xn, var_ready, std_ready, xn_ready)
            dve.wait_ge(ctx_in, 16)
            nc.vector.scalar_tensor_tensor(out=ctxsq[:], in0=ctxT[:], scalar=-0.5, in1=ctxT[:], op0=ALU.mult,
                                           op1=ALU.mult).then_inc(ctxsq_ready, 1)
            dve.wait_ge(xnT_psum, TILES // 2)
            nc.vector.tensor_copy(xnT[:, 0:512], bank[0][:]).then_inc(xnT_ready, 1)
            dve.wait_ge(ring_clear, 2)
            for n in range(TILES):
                dve.wait_ge(dot_psum, n // 2 * 2 + 2)
                dve.wait_ge(bb_ready, n + 1)
                link(nc.vector.tensor_scalar(DT[:, n, SKEW:SKEW + ROWS], bank[2 + n // 2][:, (n % 2) * ROWS:(n % 2 + 1) * ROWS],
                                             -2.0, bb[:, n:n + 1], ALU.mult, ALU.add))
                nc.vector.tensor_scalar(DT[:, n, SKEW:SKEW + ROWS], DT[:, n, SKEW:SKEW + ROWS], 0.0, None, ALU.max).then_inc(sqdist_ready, 1)

            quarter = list(range(QUAD))
            mask = [QUAD - 1] + quarter[:-1]

            def sweep_step(u, base, group, head):
                before = (u - 1) % RING
                if u % GROUP == GROUP - 1 and (not head or u == RING - 1):
                    dve.wait_ge(diff_ready, group * 2 - 4)
                if head and u == 0:
                    dve.wait_ge(ring_clear, 2)
                    dve.wait_ge(c32_in, 16)
                else:
                    dve.wait_ge(sweep, base)
                nc.vector.tensor_tensor(out=mring[:, u, :], in0=ring[:, before, 0:LANE_COLS],
                                        in1=ring[:, before, 1:LANE_COLS + 1], op=ALU.min).then_inc(sweep, 1)
                nc.vector.stream_shuffle(out=ring[:, (u + 1) % RING, 0:1], in_=ring[:, before, LANE_COLS:LANE_COLS + 1],
                                         mask=mask).then_inc(sweep, 1)
                if u % GROUP == 0:
                    dve.wait_ge(dring_ready, group + 1)
                dve.wait_ge(sweep, base + 1)
                halo = c32[:, C_FIRST:C_FIRST + 1] if head and u == 0 else ring[:, u, 0:1]
                nc.vector.tensor_tensor_scan(out=ring[:, u, 1:LANE_COLS + 1], data0=mring[:, u, :],
                                             data1=Dring[:, u, :], initial=halo, op0=ALU.min, op1=ALU.add)\
                    .then_inc(sweep, 1)

            for u in range(RING):
                sweep_step(u, 3 * u, u // GROUP, True)
            with dve.Fori(1, TURNS) as k:
                for u in range(RING):
                    sweep_step(u, k * (3 * RING) + 3 * u, k * 4 + u // GROUP, False)

            dve.wait_ge(w_lo_ready, 2 * EXPERTS)
            link(nc.vector.memset(lab[:, :, 0:1], 0.0))
            link(nc.vector.memset(entry[:, BLOCKS - 1:BLOCKS], (2 * ROWS - 1) * LABEL))
            for pr in range(BLOCK // 2):
                dve.wait_ge(masks_psum, 2 * (pr + 1))
                src = bank[pr][:].bitcast(F16)[:, 0:2 * ROWS].rearrange("p (r j) -> p r j", r=2)
                nc.vector.tensor_scalar(notleft[:, 2 * pr:2 * pr + 2, :], src, 0.0, None, ALU.is_ge)\
                    .then_inc(notleft_ready, 1)
            dve.wait_ge(c16_in, 16)
            link(nc.vector.tensor_copy(lab[:, 0, 1:ROWS + 1], half16(c16, H_LABEL)))
            for r in range(BLOCK):
                src, dst = lab[:, r % 2], lab[:, (r + 1) % 2]
                if r % 2 == 0:
                    dve.wait_ge(up_ready, r // 2 + 1)
                    dve.wait_ge(notleft_ready, r // 2 + 1)
                link(nc.vector.tensor_tensor(out=lab_t[:], in0=src[:, 1:ROWS + 1], in1=up[:, r, :], op=ALU.min))
                link(nc.vector.tensor_tensor(out=lab_e[:], in0=lab_t[:], in1=src[:, 0:ROWS], op=ALU.max))
                scan = nc.vector.tensor_tensor_scan(out=dst[:, 1:ROWS + 1], data0=notleft[:, r, :], data1=lab_e[:],
                                                    initial=0.0, op0=ALU.max, op1=ALU.min)
                if r < BLOCK - 1:
                    link(scan)
                else:
                    scan.then_inc(labels_ready, 1)
            dve.wait_ge(map_moved, 16 * BATCH)
            for k in range(BLOCKS - 1, 0, -1):
                if k < BLOCKS - 1:
                    dve.wait_ge(entries_ready, BLOCKS - 1 - k)
                nc.vector.scalar_tensor_tensor(out=junk[0:BATCH, :], in0=c16[0:BATCH, H_LABEL:H_LABEL + ROWS],
                                               scalar=entry[:, k:k + 1], in1=block_map[:, k, :],
                                               op0=ALU.is_equal, op1=ALU.mult,
                                               accum_out=entry[:, k - 1:k]).then_inc(entries_ready, 1)
            dve.wait_ge(entry_psum, 1)
            link(nc.vector.scalar_tensor_tensor(out=junk32[:], in0=bank[6][:, 0:BLOCKS], scalar=1.0,
                                                in1=c32[:, C_DIAG:C_DIAG + BLOCKS], op0=ALU.mult, op1=ALU.mult,
                                                accum_out=entry0[:]))
            dve.wait_ge(exit_ready, 1)
            for r in range(BLOCK - 1, -1, -1):
                if r == BLOCK - 1:
                    link(nc.vector.tensor_scalar(within[:, r, :], half16(c16, H_TWICE), entry0[:, 0:1], None, ALU.is_lt))
                else:
                    link(nc.vector.tensor_scalar(within[:, r, :], half16(c16, H_TWICE2), q[:, r + 1:r + 2], None,
                                                 ALU.is_lt))
                link(nc.vector.tensor_tensor_reduce(out=junk[:], in0=within[:, r, :], in1=exit2[:, r, :], scale=1.0,
                                                    scalar=0.0, op0=ALU.mult, op1=ALU.max, accum_out=q[:, r:r + 1]))
                nc.vector.scalar_tensor_tensor(out=path[:, r, :], in0=half16(c16, H_TWICE4), scalar=q[:, r:r + 1],
                                               in1=within[:, r, :], op0=ALU.is_gt, op1=ALU.mult).then_inc(path_ready, 1)
            dve.wait_ge(gate_ready, 1)
            dve.wait_ge(attn_psum, 1)
            for h in range(HALVES):
                tiles = slice(h * BATCH, (h + 1) * BATCH)
                nc.vector.scalar_tensor_tensor(out=x1[:, tiles, :], in0=bank[h][:].rearrange("p (b d) -> p b d", b=BATCH),
                                               scalar=tg[:, 0:1], in1=x[:, tiles, :], op0=ALU.mult, op1=ALU.add)\
                    .then_inc(x1_ready, 1)
            dve.wait_ge(x1_ready, HALVES)
            norm(x1, None, xn, var2_ready, std2_ready, xn2_ready)
            for h in range(HALVES):
                dve.wait_ge(xT_psum, h + 1)
                nc.vector.tensor_copy(xT[:, h * 512:(h + 1) * 512], bank[6 + h][:]).then_inc(xT_ready, 1)
                dve.wait_ge(xT_ready, h + 1)
                dve.wait_ge(xT_hi_ready, h + 1)
                nc.vector.tensor_tensor(out=xT_lo[:, h * 512:(h + 1) * 512], in0=xT[:, h * 512:(h + 1) * 512],
                                        in1=xT_hi[:, h * 512:(h + 1) * 512].bitcast(F32), op=ALU.subtract)\
                    .then_inc(xT_lo_ready, 1)

            def wide(a, n):
                return a.unsqueeze(2).to_broadcast([P, TILES, n])

            top, total_prob, inv, best, where, spare = tile1

            def ranks():
                dve.wait_ge(router_psum, 1)
                link(nc.vector.tensor_copy(logit[:], bank[6][:, 0:64].rearrange("p (n e) -> p n e", n=TILES)))
                link(nc.vector.tensor_reduce(out=top[:], in_=logit[:], axis=AX.X, op=ALU.max))
                nc.vector.tensor_tensor(out=shifted[:], in0=logit[:], in1=wide(top[:], EXPERTS), op=ALU.subtract)\
                    .then_inc(shifted_ready, 1)
                mine = logit[:].unsqueeze(3).to_broadcast([P, TILES, EXPERTS, EXPERTS])
                others = logit[:].unsqueeze(2).to_broadcast([P, TILES, EXPERTS, EXPERTS])
                earlier = c32[:, C_EARLIER:C_EARLIER + 64].rearrange("p (e o) -> p e o", e=EXPERTS)
                link(nc.vector.tensor_tensor(out=pair[:], in0=others, in1=mine, op=ALU.is_equal))
                link(nc.vector.tensor_tensor(out=pair[:], in0=pair[:],
                                             in1=earlier.unsqueeze(1).to_broadcast([P, TILES, EXPERTS, EXPERTS]),
                                             op=ALU.mult))
                link(nc.vector.tensor_tensor(out=pair2[:], in0=others, in1=mine, op=ALU.is_gt))
                link(nc.vector.tensor_tensor(out=pair[:], in0=pair[:], in1=pair2[:], op=ALU.add))
                link(nc.vector.tensor_reduce(out=rank[:], in_=pair[:], axis=AX.X, op=ALU.add))

            def counts():
                dve.wait_ge(choice_psum, 1)
                link(nc.vector.tensor_scalar(choice[:], bank[7][:, 0:64].rearrange("p (n e) -> p n e", n=TILES)[:, :, 0:MAX_K],
                                             -30.0, 30.0, ALU.max, ALU.min))
                link(nc.vector.tensor_reduce(out=best[:], in_=choice[:], axis=AX.X, op=ALU.max))
                link(nc.vector.tensor_tensor(out=first[:], in0=choice[:], in1=wide(best[:], MAX_K), op=ALU.is_equal))
                order = c32[:, C_ORDER:C_ORDER + MAX_K].unsqueeze(1).to_broadcast([P, TILES, MAX_K])
                link(nc.vector.tensor_tensor(out=first[:], in0=first[:], in1=order, op=ALU.mult))
                link(nc.vector.tensor_reduce(out=where[:], in_=first[:], axis=AX.X, op=ALU.max))
                link(nc.vector.tensor_tensor(out=rank[:], in0=rank[:], in1=wide(where[:], EXPERTS), op=ALU.add))
                link(nc.vector.tensor_scalar(rank[:], rank[:], MAX_K + 1.0, tg[:, 1:2], ALU.is_lt, ALU.mult))

            def scores():
                dve.wait_ge(exp_ready, 1)
                link(nc.vector.tensor_reduce(out=total_prob[:], in_=prob[:], axis=AX.X, op=ALU.add))
                link(nc.vector.reciprocal(inv[:], total_prob[:]))
                link(nc.vector.tensor_tensor(out=prob[:], in0=prob[:], in1=wide(inv[:], EXPERTS), op=ALU.mult))
                link(nc.vector.tensor_tensor(out=prob[:], in0=prob[:], in1=rank[:], op=ALU.mult))
                link(nc.vector.tensor_copy(score_r[:], prob[:]))
                link(nc.vector.tensor_copy(score2[:, :, 0:EXPERTS], score_r[:].bitcast(F32)))
                nc.vector.tensor_tensor(out=score2[:, :, EXPERTS:2 * EXPERTS], in0=prob[:], in1=score_r[:].bitcast(F32),
                                        op=ALU.subtract).then_inc(score_ready, 1)

            def product(v):
                dve.wait_ge(silu_ready, v + 1)
                if v >= 2:
                    dve.wait_ge(act_hi_ready, v - 1)
                    dve.wait_ge(act_lo_ready, v - 1)
                nc.vector.tensor_tensor(out=act[:, v % 2, :], in0=silu[:, v % 2, :], in1=bank[2 + v % 2][0:SUB, :],
                                        op=ALU.mult).then_inc(act_ready, 1)

            def low_part(v):
                dve.wait_ge(act_ready, v + 1)
                dve.wait_ge(act_hi_ready, v + 1)
                if v >= 2 * SUBS:
                    dve.wait_ge(down_psum, v - 2 * SUBS + 1)
                slot = v % (2 * SUBS)
                nc.vector.tensor_tensor(out=act_lo[:, slot, :], in0=act[:, v % 2, :],
                                        in1=act_hi[:, slot, :].bitcast(F32), op=ALU.subtract).then_inc(act_lo_ready, 1)

            def scale(u):
                h, e = units[u]
                dve.wait_ge(down_psum, SUBS * (u + 1))
                dve.wait_ge(wide_ready, u + 1)
                if u >= 2 and adds(u - 2):
                    dve.wait_ge(acc_ready, adds(u - 2))
                dst = scaled[:, u % 2] if e else acc[:, h]
                nc.vector.tensor_tensor(out=dst, in0=bank[4 + u % 2][:], in1=score_wide[:, u % 2], op=ALU.mult)\
                    .then_inc(scaled_ready, 1)
                if e == EXPERTS - 1:
                    dve.wait_ge(scaled_ready, u + 1)
                    dve.wait_ge(acc_ready, adds(u) - 1)
                    nc.vector.tensor_tensor(out=acc[:, h], in0=acc[:, h], in1=scaled[:, u % 2], op=ALU.add)\
                        .then_inc(acc_ready, 1)

            def finish(h):
                dve.wait_ge(acc_psum, h + 1)
                tiles = slice(h * BATCH, (h + 1) * BATCH)
                nc.vector.tensor_tensor(out=result[:, tiles, :], in0=bank[7][:].rearrange("p (b d) -> p b d", b=BATCH),
                                        in1=x1[:, tiles, :], op=ALU.add).then_inc(result_ready, 1)

            for v in range(v_turn(HALVES - 1) + 1):
                if 1 <= v <= V_TOTAL:
                    low_part(v - 1)
                if v < V_TOTAL:
                    product(v)
                if v == 1:
                    ranks()
                if v == 2:
                    counts()
                if v == 3:
                    scores()
                for u in range(UNITS):
                    if v == v_scale(u):
                        scale(u)
                for h in range(HALVES - 1):
                    if v == v_turn(h) + 1:
                        finish(h)
            finish(HALVES - 1)

        @block.tensor
        def _(pe):
            mm = nc.tensor.matmul
            pe.wait_ge(cleared, 2)
            pe.wait_ge(gates_in, 16)
            mm(bank[6][:, 0:2], ones[0:1, :], gin[:], start=True, stop=True).then_inc(gate_psum, 1)
            pe.wait_ge(c32_in, 16)
            for n in range(TILES):
                pe.wait_ge(xn_ready, n + 1)
                nc.tensor.transpose(bank[n // 4][:, (n % 4) * P:(n % 4 + 1) * P], xn[:, n, :], ident).then_inc(xnT_psum, 1)
            pe.wait_ge(ctxsq_ready, 1)
            pe.wait_ge(xnT_ready, 2)
            for n in range(TILES):
                b = n % BATCH
                dst = bank[2 + n // 2][:, (n % 2) * ROWS:(n % 2 + 1) * ROWS]
                mm(dst, xnT[:, n * P:(n + 1) * P], ctxT[:, b * ROWS:(b + 1) * ROWS], start=True, stop=False)
                mm(dst, ones[:], ctxsq[:, b * ROWS:(b + 1) * ROWS], start=False, stop=True).then_inc(dot_psum, 1)
            pe.wait_ge(c16_in, 16)
            pe.wait_ge(masks_moved, 16 * 2 * HALVES * len(CHUNK_ENDS))
            pe.wait_ge(sqdist_ready, TILES)
            pe.wait_ge(xnT_ready, 2)
            for r in range(BLOCK):
                for plane in range(2):
                    for h in range(HALVES):
                        at = (r % 2) * ROWS + h * P
                        src = KT[:, h, plane].rearrange("p b (k r) -> p (b k) r", r=BLOCK)[:, :, r]
                        last = nc.tensor.transpose(bank[plane * 4 + r // 2][:].bitcast(F16)[:, at:at + P], src, ident16)
                last.then_inc(masks_psum, 1)
            pe.wait_ge(entries_ready, BLOCKS - 1)
            pe.wait_ge(gate_ready, 1)
            mm(bank[6][:, 0:BLOCKS], c32[0:BATCH, C_BATCH:C_BATCH + P], entry[:], start=True, stop=True)\
                .then_inc(entry_psum, 1)
            pe.wait_ge(ctx_hi_ready, 1 + BATCH)
            pe.wait_ge(ctx_lo_ready, BATCH)
            pe.wait_ge(up_ready, BLOCK // 2)
            pe.wait_ge(notleft_ready, BLOCK // 2)
            for i, r in enumerate(range(BLOCK - 1, -1, -1)):
                pe.wait_ge(path_ready, i + 1)
                for h in range(HALVES):
                    tok = path[:, r, h * P:(h + 1) * P]
                    mm(bank[h][:], tok, ctx_hi[:, r], start=(i == 0), stop=False)
                    last = mm(bank[h][:], tok, ctx_lo[:, r], start=False, stop=(i == BLOCK - 1))
            last.then_inc(attn_psum, 1)
            for n in range(TILES):
                pe.wait_ge(xn2_ready, n + 1)
                last = nc.tensor.transpose(bank[6 + n // 4][:, (n % 4) * P:(n % 4 + 1) * P], xn[:, n, :], ident)
                if n % 4 == 3:
                    last.then_inc(xT_psum, 1)

            def split_mm(dst, w_hi, w_lo, a_hi, a_lo, start, stop):
                mm(dst, w_hi, a_hi, start=start, stop=False)
                mm(dst, w_hi, a_lo, start=False, stop=False)
                return mm(dst, w_lo, a_hi, start=False, stop=stop)

            def gate_up(v):
                h, e = units[v // SUBS]
                m = v % SUBS
                if v % (SUBS * EXPERTS) == 0:
                    pe.wait_ge(xT_lo_ready, h + 1)
                    pe.wait_ge(xT_hi_ready, h + 1)
                if v >= 2:
                    pe.wait_ge(act_ready, v - 1)
                tok = slice(h * 512, (h + 1) * 512)
                for part in range(2):
                    col = slice(m * SUB, (m + 1) * SUB)
                    last = split_mm(bank[2 * part + v % 2][0:SUB, :], gu_hi[:, e, part, col], gu_lo[:, e, part, col],
                                    xT_hi[:, tok], xT_lo[:, tok], True, True)
                last.then_inc(gu_psum, 1)

            def down(v):
                u, m = v // SUBS, v % SUBS
                h, e = units[u]
                pe.wait_ge(act_hi_ready, v + 1)
                pe.wait_ge(act_lo_ready, v + 1)
                if m == 0 and u >= 2:
                    pe.wait_ge(scaled_ready, u - 1)
                slot, col = v % (2 * SUBS), slice(m * DIM, (m + 1) * DIM)
                split_mm(bank[4 + u % 2][:], dn_hi[:, e, col], dn_lo[:, e, col], act_hi[:, slot, :], act_lo[:, slot, :],
                         m == 0, m == SUBS - 1).then_inc(down_psum, 1)

            def router_actor():
                pe.wait_ge(router_in, 80)
                pe.wait_ge(xT_ready, HALVES)
                pe.wait_ge(xT_hi_ready, HALVES)
                for h in range(HALVES):
                    mm(bank[4 + h][0:ACTOR, :], wa1[:], xT[:, h * 512:(h + 1) * 512], start=True, stop=True)\
                        .then_inc(actor_psum, 1)
                for n in range(TILES):
                    last = mm(bank[6][:, n * EXPERTS:(n + 1) * EXPERTS], xT[:, n * P:(n + 1) * P], wr[:],
                              start=True, stop=True)
                last.then_inc(router_psum, 1)
                pe.wait_ge(actor_ready, HALVES)
                for n in range(TILES):
                    dst = bank[7][:, n * EXPERTS:n * EXPERTS + MAX_K]
                    mm(dst, actor[:, n * P:(n + 1) * P], wa2[:], start=True, stop=False)
                    last = mm(dst, ones[0:1, :], ba2[:], start=False, stop=True)
                last.then_inc(choice_psum, 1)

            pe.wait_ge(w_lo_ready, 2 * EXPERTS)
            for v in range(v_turn(HALVES - 1) + 1):
                if v < V_TOTAL:
                    gate_up(v)
                if 2 <= v < V_TOTAL + 2:
                    down(v - 2)
                if v == 1:
                    router_actor()
                if v == V_SCORES:
                    pe.wait_ge(score_ready, 1)
                    for h in range(HALVES):
                        for b in range(BATCH):
                            last = nc.tensor.transpose(bank[6 + h][0:2 * EXPERTS, b * P:(b + 1) * P],
                                                       score2[:, h * BATCH + b, :], ident)
                        last.then_inc(scoreT_psum, 1)
                for u in range(UNITS):
                    if v == v_wide(u):
                        if u:
                            pe.wait_ge(wide_ready, u)
                        else:
                            pe.wait_ge(scoreT_ready, HALVES)
                            pe.wait_ge(pick_ready, 1)
                        h, e = units[u]
                        mm(bank[6][:], pick[:, e, :], scoreT[:, h * 512:(h + 1) * 512], start=True, stop=True)\
                            .then_inc(wide_psum, 1)
                for h in range(HALVES):
                    if v == v_turn(h):
                        pe.wait_ge(acc_ready, adds((h + 1) * EXPERTS - 1))
                        if h:
                            pe.wait_ge(result_ready, h)
                        for b in range(BATCH):
                            last = nc.tensor.transpose(bank[7][:, b * P:(b + 1) * P], acc[:, h, b * P:(b + 1) * P], ident)
                        last.then_inc(acc_psum, 1)


def constants():
    import numpy as np

    c32 = np.zeros((P, C_WIDTH), np.float32)
    p = np.arange(P)
    c32[p, C_IDENT + p] = 1
    c32[p, C_DIAG + p % BLOCKS] = 1
    c32[p // BLOCKS, C_BATCH + p] = 1
    e = np.arange(EXPERTS)
    c32[:, C_EARLIER:C_EARLIER + 64] = (e[None, :] < e[:, None]).reshape(-1)
    c32[:, C_ORDER:C_ORDER + MAX_K] = MAX_K - np.arange(MAX_K)
    c32[p, C_MINE + p // QUAD] = 1
    c32[p, C_PICK + p % EXPERTS] = 1
    c32[:, C_FIRST] = np.where(p % QUAD == 0, 0.0, FAR)
    c16 = np.zeros((P, H_WIDTH), np.float16)
    c16[p, H_IDENT + p] = 1
    j = np.arange(ROWS)
    for at, v in ((H_LABEL, 2 * j + 1), (H_TWICE, 2 * j), (H_TWICE2, 2 * j + 2), (H_TWICE4, 2 * j + 4)):
        c16[:, at:at + ROWS] = v * LABEL
    return c32, c16


def kernel(x, ctx_1024, g_xattn, g_ffn, L0_ffn_router_w, L0_ffn_actor_w1, L0_ffn_actor_b1, L0_ffn_actor_w2,
           L0_ffn_actor_b2, L0_ffn_gate_w, L0_ffn_up_w, L0_ffn_down_w):
    import numpy as np
    import concourse.bacc as bacc
    from concourse.bass_utils import run_bass_kernel_spmd

    a = np.asarray
    c32, c16 = constants()
    arrays = {
        "x_tok": a(x).reshape(BATCH, HALVES, P, DIM).transpose(2, 1, 0, 3).reshape(P, TILES, DIM),
        "ctx_t": a(ctx_1024).reshape(BATCH * ROWS, DIM).T,
        "ctx_blk": a(ctx_1024).reshape(BATCH * BLOCKS, BLOCK, DIM),
        "gates": np.concatenate([a(g_xattn), a(g_ffn)]).reshape(1, 2),
        "w_gate": a(L0_ffn_gate_w).transpose(2, 0, 1),
        "w_up": a(L0_ffn_up_w).transpose(2, 0, 1),
        "w_down": a(L0_ffn_down_w).reshape(EXPERTS, DIM, SUBS, SUB).transpose(3, 0, 2, 1).reshape(SUB, EXPERTS, SUBS * DIM),
        "w_router": a(L0_ffn_router_w).T,
        "w_a1": a(L0_ffn_actor_w1).T,
        "b_a1": a(L0_ffn_actor_b1).reshape(ACTOR, 1),
        "w_a2": a(L0_ffn_actor_w2).T,
        "b_a2": a(L0_ffn_actor_b2).reshape(1, MAX_K),
        "const32": c32,
        "const16": c16,
    }
    arrays = {k: np.ascontiguousarray(v) for k, v in arrays.items()}
    nc = bacc.Bacc("TRN2", target_bir_lowering=False, num_devices=1)
    aps = [nc.dram_tensor(k, v.shape, mybir.dt.from_np(v.dtype), kind="ExternalInput").ap() for k, v in arrays.items()]
    out = nc.dram_tensor("out", (P, HALVES, BATCH, DIM), mybir.dt.float32, kind="ExternalOutput").ap()
    dist_dram = nc.dram_tensor("dist_dram", (BATCH * ROWS, D_WIDTH), mybir.dt.float32, kind="Internal").ap()
    mask_dram = nc.dram_tensor("mask_dram", (BATCH, ROWS, 2, M_WIDTH), mybir.dt.float16, kind="Internal").ap()
    build(nc, *aps, dist_dram, mask_dram, out)
    r = run_bass_kernel_spmd(nc, [arrays], core_ids=[0])
    got = a(r.results[0]["out"])
    return got.transpose(2, 1, 0, 3).reshape(BATCH, ROWS, DIM)
```

```python
from contextlib import ExitStack

import concourse.bass as bass
from concourse import mybir

BATCH, ROWS, DIM = 4, 256, 128
EXPERTS, INNER, MAX_K, ACTOR = 8, 336, 6, 50
P = 128
TILES = BATCH * ROWS // P
HALVES = ROWS // P
LANE_COLS = 16
LANES = ROWS // LANE_COLS
QUAD = 32
LAG = 2
GROUP = 8
RING = 4 * GROUP
STEPS = 288
GROUPS = STEPS // GROUP
TURNS = STEPS // RING
BLOCK = 8
BLOCKS = ROWS // BLOCK
CHUNK_ENDS = [96, 192, 240, 256]
CHUNKS = len(CHUNK_ENDS)
SKEW = LAG * (LANES - 1)
D_WIDTH = ROWS + 2 * SKEW + 4
M_PAD = 32
M_WIDTH = STEPS + M_PAD + 8
SUB = 112
SUBS = INNER // SUB
HALF_TOKENS = BATCH * P
FAR = 1e30
LABEL = 1.0 / 1024
ACTOR_PAD = 64
MASKS_BY_SP = 3
DMA_BLOCKS = 24
LOADS_BY_SP = 2

DOWN_LAG = 3
UNITS = HALVES * EXPERTS
V_TOTAL = UNITS * SUBS
V_SCORES = 4


def v_wide(u):
    return max(SUBS * u + DOWN_LAG + 1, V_SCORES + 1)


def v_scale(u):
    return max(SUBS * u + DOWN_LAG + 3, V_SCORES + 2)


def v_part(h):
    return v_scale((h + 1) * EXPERTS - 2) + (2 if h == HALVES - 1 else 3)


def v_turn(h):
    return v_scale((h + 1) * EXPERTS - 1) + (0 if h == HALVES - 1 else 2)


def adds(u):
    return u - u // EXPERTS - (u + 1) // EXPERTS

C_IDENT, C_DIAG, C_BATCH, C_EARLIER, C_ORDER, C_FIRST, C_MINE, C_PICK = 0, 128, 160, 288, 352, 360, 361, 365
C_WIDTH = 373
H_IDENT, H_LABEL, H_TWICE, H_TWICE2, H_TWICE4 = 0, 128, 384, 640, 896
H_WIDTH = 1152


def build(nc, x_tok, ctx_t, ctx_blk, gates, w_gate, w_up, w_down, w_router, w_a1, b_a1, w_a2, b_a2,
          const32, const16, dist_dram, mask_dram, out):
    F32, F16, F32R = mybir.dt.float32, mybir.dt.float16, mybir.dt.float32r
    ALU, ACT, AX = mybir.AluOpType, mybir.ActivationFunctionType, mybir.AxisListType

    with ExitStack() as stack:
        def sb(name, shape, dtype=F32):
            return stack.enter_context(nc.sbuf_tensor(name, shape, dtype))

        def sem(name):
            return stack.enter_context(nc.semaphore(name))

        x = sb("x", [P, TILES, DIM])
        c32 = sb("c32", [P, C_WIDTH])
        c16 = sb("c16", [P, H_WIDTH], F16)
        ones = sb("ones", [P, P])
        warm_in, warm_w = sb("warm_in", [P, 512], F16), sb("warm_w", [P, P], F16)
        gin = sb("gin", [1, 2])
        tg = sb("tg", [P, 2])
        stats = sb("stats", [P, TILES, 6])
        mv = sb("mv", [P, TILES, 2])
        var = sb("var", [P, TILES])
        std = sb("std", [P, TILES])
        rstd = sb("rstd", [P, TILES])
        xn = sb("xn", [P, TILES, DIM])
        bb = sb("bb", [P, TILES])
        entry = sb("entry", [BATCH, BLOCKS])
        gu_hi = sb("gu_hi", [P, EXPERTS, 2, INNER], F32R)
        dn_hi = sb("dn_hi", [SUB, EXPERTS, SUBS * DIM], F32R)
        with nc.sbuf_tensor("gu_w", [P, EXPERTS, 2, INNER], F32) as gu_w, \
                nc.sbuf_tensor("dn_w", [SUB, EXPERTS, SUBS * DIM], F32) as dn_w:
            pass
        gu_lo = sb("gu_lo", [P, EXPERTS, 2, INNER], F32R)
        dn_lo = sb("dn_lo", [SUB, EXPERTS, SUBS * DIM], F32R)
        wr = sb("wr", [P, EXPERTS])
        wa1 = sb("wa1", [P, ACTOR])
        ba1 = sb("ba1", [ACTOR, 1])
        wa2 = sb("wa2", [ACTOR + 1, MAX_K])

        pick = sb("pick", [2 * EXPERTS, EXPERTS, P], F32R)

        alignment = ExitStack()

        def sb(name, shape, dtype=F32):
            return alignment.enter_context(nc.sbuf_tensor(name, shape, dtype))

        KT = sb("KT", [P, HALVES, 2, BATCH, ROWS], F16)
        ctxb = sb("ctxb", [P, BLOCK, DIM])
        ctx_part = sb("ctx_part", [P, BLOCK, DIM], F32R)
        ctx_hi = sb("ctx_hi", [P, BLOCK, BATCH, DIM], F32R)
        ctx_lo = sb("ctx_lo", [P, BLOCK, BATCH, DIM], F32R)

        early = ExitStack()

        def sb(name, shape, dtype=F32):
            return early.enter_context(nc.sbuf_tensor(name, shape, dtype))

        ctxT = sb("ctxT", [P, BATCH * ROWS])
        ctxsq = sb("ctxsq", [P, BATCH * ROWS])
        ctxsum = sb("ctxsum", [P, BATCH * ROWS])
        sq_junk = sb("sq_junk", [P, DIM])
        xnT = sb("xnT", [P, TILES * P])
        DT = sb("DT", [P, TILES, D_WIDTH])
        Dk = sb("Dk", [P, LANE_COLS, STEPS])
        Dring = sb("Dring", [P, RING, LANE_COLS])
        ring = sb("ring", [P, RING, LANE_COLS + 1])
        mring = sb("mring", [P, RING, LANE_COLS])
        diff = sb("diff", [P, 2, 2, GROUP, LANE_COLS])
        K = sb("K", [P, LANE_COLS, 2, STEPS + 2], F16)
        early.close()

        def sb(name, shape, dtype=F32):
            return alignment.enter_context(nc.sbuf_tensor(name, shape, dtype))

        notleft = sb("notleft", [P, BLOCK, ROWS], F16)
        up = sb("up", [P, BLOCK, ROWS], F16)
        exit2 = sb("exit2", [P, BLOCK, ROWS], F16)
        upsum = sb("upsum", [P, BLOCK, ROWS], F16)
        lab = sb("lab", [P, 2, ROWS + 1], F16)
        lab_t = sb("lab_t", [P, ROWS], F16)
        lab_e = sb("lab_e", [P, ROWS], F16)
        block_map = sb("block_map", [BATCH, DMA_BLOCKS, ROWS], F16)
        junk = sb("junk", [P, ROWS])
        entry0 = sb("entry0", [P, 1])
        junk32 = sb("junk32", [P, BLOCKS])
        within = sb("within", [P, BLOCK, ROWS], F16)
        q = sb("q", [P, BLOCK])
        path = sb("path", [P, BLOCK, ROWS], F32R)
        alignment.close()

        def sb(name, shape, dtype=F32):
            return stack.enter_context(nc.sbuf_tensor(name, shape, dtype))

        x1 = sb("x1", [P, TILES, DIM])
        xT = sb("xT", [P, TILES * P])
        xT_hi = sb("xT_hi", [P, TILES * P], F32R)
        xT_lo = sb("xT_lo", [P, TILES * P], F32R)
        actor = sb("actor", [ACTOR_PAD, TILES * P])
        logit = sb("logit", [P, TILES, EXPERTS])
        shifted = sb("shifted", [P, TILES, EXPERTS])
        prob = sb("prob", [P, TILES, EXPERTS])
        tile1 = [sb(f"tile1_{i}", [P, TILES]) for i in range(6)]
        pair = sb("pair", [P, TILES, EXPERTS, EXPERTS])
        pair2 = sb("pair2", [P, TILES, EXPERTS, EXPERTS])
        rank = sb("rank", [P, TILES, EXPERTS])
        choice = sb("choice", [P, TILES, MAX_K])
        first = sb("first", [P, TILES, MAX_K])
        silu = sb("silu", [SUB, 2, HALF_TOKENS])
        act = sb("act", [SUB, 2, HALF_TOKENS])
        act_hi = sb("act_hi", [SUB, 2 * SUBS, HALF_TOKENS], F32R)
        act_lo = sb("act_lo", [SUB, 2 * SUBS, HALF_TOKENS], F32R)
        score_r = sb("score_r", [P, TILES, EXPERTS], F32R)
        score2 = sb("score2", [P, TILES, 2 * EXPERTS])
        scoreT = sb("scoreT", [2 * EXPERTS, TILES * P], F32R)
        score_wide = sb("score_wide", [P, 2, HALF_TOKENS])
        scaled = sb("scaled", [P, 2, HALF_TOKENS])
        acc = sb("acc", [P, HALVES, HALF_TOKENS])
        result = sb("result", [P, TILES, DIM])
        bank = [stack.enter_context(nc.psum_tensor(f"bank{i}", [P, 512], F32)) for i in range(8)]

        x_in, ctx_in, c32_in, c16_in, ctxb_in = map(sem, ("x_in", "ctx_in", "c32_in", "c16_in", "ctxb_in"))
        gates_in, weights_in, router_in = map(sem, ("gates_in", "weights_in", "router_in"))
        cleared = sem("cleared")
        ring_clear = sem("ring_clear")
        dve_step = sem("dve_step")
        var_ready, std_ready, xn_ready = map(sem, ("var_ready", "std_ready", "xn_ready"))
        bb_ready, xnT_psum, xnT_ready, ctxsq_ready = map(sem, ("bb_ready", "xnT_psum", "xnT_ready", "ctxsq_ready"))
        ctxsum_psum, ctxsum_ready, act_step = map(sem, ("ctxsum_psum", "ctxsum_ready", "act_step"))
        warm_clear, crossed = sem("warm_clear"), sem("crossed")
        warm = sem("warm")
        gate_psum, gate_ready = map(sem, ("gate_psum", "gate_ready"))
        dot_psum, sqdist_ready, dist_ready = map(sem, ("dot_psum", "sqdist_ready", "dist_ready"))
        dist_stored = [sem(f"dist_stored_{h}") for h in range(HALVES)]
        lanes_in = [sem(f"lanes_in_{h}") for h in range(HALVES)]
        lanes_in_pool = [sem(f"lanes_in_pool_{h}") for h in range(HALVES)]
        masks_stored, masks_stored_pool = sem("masks_stored"), sem("masks_stored_pool")
        dring_ready = sem("dring_ready")
        sweep = sem("sweep")
        diff_ready = sem("diff_ready")
        signs_ready = sem("signs_ready")
        masks_moved = sem("masks_moved")
        w_hi_ready, w_lo_ready = sem("w_hi_ready"), sem("w_lo_ready")
        masks_psum, notleft_ready, up_ready, exit_ready = map(sem, ("masks_psum", "notleft_ready", "up_ready", "exit_ready"))
        up_label_ready, upsum_ready = sem("up_label_ready"), sem("upsum_ready")
        labels_ready, map_moved, map_psum, entries_ready = map(sem, ("labels_ready", "map_moved", "map_psum", "entries_ready"))
        entry_psum, path_ready, attn_psum, x1_ready = map(sem, ("entry_psum", "path_ready", "attn_psum", "x1_ready"))
        var2_ready, std2_ready, xn2_ready = map(sem, ("var2_ready", "std2_ready", "xn2_ready"))
        xT_psum, xT_ready, xT_hi_ready, xT_lo_ready = map(sem, ("xT_psum", "xT_ready", "xT_hi_ready", "xT_lo_ready"))
        router_psum, actor_psum, actor_ready, choice_psum = map(sem, ("router_psum", "actor_psum", "actor_ready", "choice_psum"))
        shifted_ready, exp_ready = sem("shifted_ready"), sem("exp_ready")
        gu_psum, silu_ready, act_ready, act_hi_ready, act_lo_ready = map(
            sem, ("gu_psum", "silu_ready", "act_ready", "act_hi_ready", "act_lo_ready"))
        down_psum, scaled_ready, acc_ready, out_done = map(sem, ("down_psum", "scaled_ready", "acc_ready", "out_done"))
        ctx_hi_ready, ctx_low, ctx_lo_ready = map(sem, ("ctx_hi_ready", "ctx_low", "ctx_lo_ready"))
        pick_ready, score_ready, scoreT_psum, scoreT_ready = map(
            sem, ("pick_ready", "score_ready", "scoreT_psum", "scoreT_ready"))
        wide_psum, wide_ready = sem("wide_psum"), sem("wide_ready")
        actor_ones = sem("actor_ones")
        acc_psum, partial_ready, last_psum, result_ready = map(sem, ("acc_psum", "partial_ready", "last_psum", "result_ready"))
        stack.enter_context(nc.allow_non_contiguous_dma(reason="single columns of small operands"))
        block = stack.enter_context(nc.Block())

        ident = c32[:, C_IDENT:C_IDENT + P]
        ident16 = c16[:, H_IDENT:H_IDENT + P]

        def half16(t, at):
            return t[:, at:at + ROWS]

        units = [(h, e) for h in range(HALVES) for e in range(EXPERTS)]

        def lanes_load(h, b):
            lane0, step0 = h * LANES // HALVES, h * LAG * LANES // HALVES
            src = bass.AP(dist_dram.tensor, b * ROWS * D_WIDTH + lane0 * (LANE_COLS * D_WIDTH - LAG) + SKEW + step0,
                          [[LANE_COLS * D_WIDTH - LAG, LANES // HALVES], [D_WIDTH, LANE_COLS], [1, STEPS - step0]])
            lanes = slice(b * QUAD + lane0, b * QUAD + lane0 + LANES // HALVES)
            return Dk[lanes, :, step0:STEPS], src

        def chunk_steps(chunk):
            groups_to = [0] + [-(-(end + SKEW) // GROUP) for end in CHUNK_ENDS]
            return [0 if not g else g * GROUP + 1 for g in groups_to[chunk:chunk + 2]] + [groups_to[chunk + 1]]

        def mask_store(chunk, b):
            sent, upto, _ = chunk_steps(chunk)
            dst = bass.AP(mask_dram.tensor, b * 2 * ROWS * M_WIDTH + sent + M_PAD - 1,
                          [[2 * LANE_COLS * M_WIDTH - LAG, LANES], [M_WIDTH, 2 * LANE_COLS], [1, upto - sent]])
            return dst, K[b * QUAD:b * QUAD + LANES, :, :, sent:upto].rearrange("c j m t -> c (j m) t")

        def mask_load(chunk, h, plane):
            begin, end = ([0] + CHUNK_ENDS)[chunk:chunk + 2]
            src = bass.AP(mask_dram.tensor, (h * P * 2 + plane) * M_WIDTH + M_PAD + begin,
                          [[2 * M_WIDTH, P], [2 * ROWS * M_WIDTH, BATCH], [1, end - begin]])
            return KT[:, h, plane, :, begin:end], src

        @block.sync
        def _(sp):
            sp.dma_start(x[:], x_tok).then_inc(x_in, 16)
            sp.dma_start(c32[:], const32).then_inc(c32_in, 16)
            sp.dma_start(gin[:], gates).then_inc(gates_in, 16)
            for h in range(HALVES):
                sp.wait_ge(dist_ready, BATCH * (h + 1))
                sp.dma_start(bass.AP(dist_dram.tensor, h * P * D_WIDTH,
                                     [[D_WIDTH, P], [ROWS * D_WIDTH, BATCH], [1, D_WIDTH]]),
                             DT[:, h * BATCH:(h + 1) * BATCH, :]).then_inc(dist_stored[h], 16)
            for h in range(HALVES):
                sp.wait_ge(dist_stored[h], 16)
                sp.wait_ge(cleared, 2)
                for b in range(LOADS_BY_SP):
                    sp.dma_start(*lanes_load(h, b)).then_inc(lanes_in[h], 16)
            sp.dma_start(c16[:], const16).then_inc(c16_in, 16)
            sp.dma_start(ctxb[:], ctx_blk).then_inc(ctxb_in, 16)
            sp.dma_start(gu_w[:, :, 0, :], w_gate).then_inc(weights_in, 16)
            sp.dma_start(gu_w[:, :, 1, :], w_up).then_inc(weights_in, 16)
            sp.dma_start(dn_w[:], w_down).then_inc(weights_in, 16)
            for dst, src in ((wr[:], w_router), (wa1[:], w_a1), (ba1[:], b_a1), (wa2[0:ACTOR, :], w_a2),
                             (wa2[ACTOR:ACTOR + 1, :], b_a2)):
                sp.dma_start(dst, src).then_inc(router_in, 16)
            for chunk in range(CHUNKS):
                last = chunk == CHUNKS - 1
                groups = chunk_steps(chunk)[2]
                batches = MASKS_BY_SP if last else BATCH
                sp.wait_ge(signs_ready, 2 * groups)
                for b in range(batches):
                    sp.dma_start(*mask_store(chunk, b)).then_inc(masks_stored, 16)
                sp.wait_ge(masks_stored, 16 * (BATCH * chunk + batches))
                if last:
                    sp.wait_ge(masks_stored_pool, 16 * (BATCH - batches))
                for h in range(HALVES):
                    for plane in range(2):
                        sp.dma_start(*mask_load(chunk, h, plane)).then_inc(masks_moved, 16)
            sp.wait_ge(labels_ready, 1)
            for b in range(BATCH):
                sp.dma_start(block_map[b:b + 1, :, :], lab[b * BLOCKS:b * BLOCKS + DMA_BLOCKS, 0, 1:ROWS + 1])\
                  .then_inc(map_moved, 16)
            for h in range(HALVES):
                sp.wait_ge(result_ready, h + 1)
                sp.dma_start(out[:, h], result[:, h * BATCH:(h + 1) * BATCH, :]).then_inc(out_done, 16)
            sp.wait_ge(out_done, 16 * HALVES)

        @block.gpsimd
        def _(pool):
            nc.gpsimd.memset(warm_in[:], 0.0).then_inc(warm_clear, 1)
            nc.gpsimd.memset(warm_w[:], 0.0).then_inc(warm_clear, 1)
            nc.gpsimd.memset(ones[:], 1.0).then_inc(cleared, 1)
            nc.gpsimd.memset(Dk[:], FAR).then_inc(cleared, 1)
            nc.gpsimd.memset(K[:, :, :, 0:2], 0.0).then_inc(cleared, 1)
            for h in range(HALVES):
                pool.wait_ge(dist_stored[h], 16)
                pool.wait_ge(cleared, 2)
                for b in range(LOADS_BY_SP, BATCH):
                    pool.dma_start(*lanes_load(h, b)).then_inc(lanes_in_pool[h], 16)

            def group_diffs(q_, group, head):
                s = q_ * GROUP
                pool.wait_ge(sweep, 3 * GROUP * (group + 1))
                if not head or q_ >= 2:
                    pool.wait_ge(signs_ready, group * 2 - 2)
                left = ring[:, s:s + GROUP, 0:LANE_COLS]
                nc.gpsimd.tensor_tensor(out=diff[:, q_ % 2, 0], in0=left, in1=mring[:, s:s + GROUP, :],
                                        op=ALU.subtract).then_inc(diff_ready, 1)
                nc.gpsimd.tensor_tensor(out=diff[:, q_ % 2, 1], in0=left, in1=ring[:, s:s + GROUP, 1:LANE_COLS + 1],
                                        op=ALU.subtract).then_inc(diff_ready, 1)

            for q_ in range(4):
                group_diffs(q_, q_, True)
            pool.wait_ge(ctx_hi_ready, 1)
            nc.gpsimd.tensor_tensor(out=ctxb[:], in0=ctxb[:], in1=ctx_part[:].bitcast(F32), op=ALU.subtract)\
                .then_inc(ctx_low, 1)
            with pool.Fori(1, TURNS) as k:
                pool.wait_ge(w_hi_ready, k * 2)
                nc.gpsimd.tensor_tensor(out=gu_lo[:, bass.ds(k - 1, 1)], in0=gu_w[:, bass.ds(k - 1, 1)],
                                        in1=gu_hi[:, bass.ds(k - 1, 1)].bitcast(F32), op=ALU.subtract)\
                    .then_inc(w_lo_ready, 1)
                nc.gpsimd.tensor_tensor(out=dn_lo[:, bass.ds(k - 1, 1)], in0=dn_w[:, bass.ds(k - 1, 1)],
                                        in1=dn_hi[:, bass.ds(k - 1, 1)].bitcast(F32), op=ALU.subtract)\
                    .then_inc(w_lo_ready, 1)
                for q_ in range(4):
                    group_diffs(q_, k * 4 + q_, False)
            pool.wait_ge(signs_ready, 2 * GROUPS)
            for b in range(MASKS_BY_SP, BATCH):
                pool.dma_start(*mask_store(CHUNKS - 1, b)).then_inc(masks_stored_pool, 16)
            pool.wait_ge(up_label_ready, 1)
            pool.wait_ge(c16_in, 16)
            nc.gpsimd.tensor_tensor(out=upsum[:], in0=upsum[:],
                                    in1=half16(c16, H_TWICE2).unsqueeze(1).to_broadcast([P, BLOCK, ROWS]),
                                    op=ALU.add).then_inc(upsum_ready, 1)
            pool.wait_ge(upsum_ready, 1)
            pool.wait_ge(notleft_ready, BLOCK // 2)
            nc.gpsimd.tensor_tensor(out=exit2[:], in0=upsum[:], in1=notleft[:], op=ALU.mult).then_inc(exit_ready, 1)
            pool.wait_ge(x1_ready, HALVES)
            nc.gpsimd.memset(actor[32:ACTOR_PAD, :], 1.0).then_inc(actor_ones, 1)
            for u in range(UNITS):
                h, e = units[u]
                if 0 < e < EXPERTS - 1:
                    pool.wait_ge(scaled_ready, u + 1)
                    if e > 1:
                        pool.wait_ge(acc_ready, adds(u) - 1)
                    nc.gpsimd.tensor_tensor(out=acc[:, h], in0=acc[:, h], in1=scaled[:, u % 2], op=ALU.add)\
                        .then_inc(acc_ready, 1)

        @block.scalar
        def _(sc):
            sc.dma_start(ctxT[:], ctx_t).then_inc(ctx_in, 16)
            sc.wait_ge(cleared, 1)
            nc.scalar.activation(std[:], ones[:, 0:TILES], ACT.Sqrt).then_inc(act_step, 1)
            sc.wait_ge(act_step, 1)
            sc.wait_ge(var_ready, 1)
            nc.scalar.activation(std[:], var[:], ACT.Sqrt).then_inc(std_ready, 1)
            sc.wait_ge(ctx_in, 16)
            nc.scalar.activation(ctxsq[:], ctxT[:], ACT.Square).then_inc(ctxsq_ready, 1)

            def token_squares(h):
                for n in range(h * BATCH, (h + 1) * BATCH):
                    sc.wait_ge(xn_ready, n + 1)
                    if n:
                        sc.wait_ge(bb_ready, n)
                    nc.scalar.activation(sq_junk[:], xn[:, n, :], ACT.Square, accum_out=bb[:, n:n + 1]).then_inc(bb_ready, 1)

            token_squares(0)
            for h in range(HALVES):
                sc.wait_ge(xnT_psum, BATCH * (h + 1))
                nc.scalar.activation(xnT[:, h * 512:(h + 1) * 512], bank[h][:], ACT.Copy).then_inc(xnT_ready, 1)
            for h in range(2):
                sc.wait_ge(ctxsum_psum, h + 1)
                nc.scalar.activation(ctxsum[:, h * 512:(h + 1) * 512], bank[6 + h][:], ACT.Copy).then_inc(ctxsum_ready, 1)
            token_squares(1)
            for n in range(TILES):
                sc.wait_ge(sqdist_ready, n + 1)
                nc.scalar.activation(DT[:, n, SKEW:SKEW + ROWS], DT[:, n, SKEW:SKEW + ROWS], ACT.Sqrt).then_inc(dist_ready, 1)

            def dist_group(slot, group_start):
                nc.scalar.activation(Dring[:, slot * GROUP:(slot + 1) * GROUP, :].rearrange("p t j -> p j t"),
                                     Dk[:, :, group_start], ACT.Copy).then_inc(dring_ready, 1)

            def sign_group(half, own, after):
                for plane, cols in ((0, own), (1, after)):
                    nc.scalar.activation(K[:, :, plane, cols], diff[:, half, plane].rearrange("p t j -> p j t"), ACT.Sign)\
                        .then_inc(signs_ready, 1)

            for g in range(4):
                for h in range(1 if g < LAG * LANES // HALVES // GROUP else HALVES):
                    sc.wait_ge(lanes_in[h], 16 * LOADS_BY_SP)
                    sc.wait_ge(lanes_in_pool[h], 16 * (BATCH - LOADS_BY_SP))
                dist_group(g, slice(g * GROUP, (g + 1) * GROUP))
            sc.wait_ge(ctxb_in, 16)
            sc.wait_ge(c32_in, 16)
            nc.scalar.activation(ctx_part[:], ctxb[:], ACT.Copy).then_inc(ctx_hi_ready, 1)
            sc.wait_ge(ctx_hi_ready, 1)
            for b in range(BATCH):
                nc.scalar.activation(ctx_hi[:, :, b, :], ctx_part[:].bitcast(F32), ACT.Copy,
                                     scale=c32[:, C_MINE + b:C_MINE + b + 1]).then_inc(ctx_hi_ready, 1)
            nc.scalar.activation(pick[:], c32[0:2 * EXPERTS, C_PICK:C_PICK + EXPERTS].unsqueeze(2)
                                 .to_broadcast([2 * EXPERTS, EXPERTS, P]), ACT.Copy).then_inc(pick_ready, 1)
            sc.wait_ge(gate_psum, 1)
            nc.scalar.activation(tg[:], bank[1][:, 0:2], ACT.Tanh).then_inc(gate_ready, 1)
            sc.wait_ge(cleared, 3)
            with sc.Fori(0, TURNS - 1) as k:
                for s in range(4):
                    sc.wait_ge(sweep, k * (12 * GROUP) + 3 * GROUP * (s + 1))
                    dist_group(s, bass.ds(k * RING + (RING + s * GROUP), GROUP))
                    sc.wait_ge(diff_ready, k * 8 + 2 * (s + 1))
                    sign_group(s % 2, bass.ds(k * RING + (s * GROUP + 1), GROUP), bass.ds(k * RING + (s * GROUP + 2), GROUP))
                sc.wait_ge(weights_in, 48)
                nc.scalar.activation(gu_hi[:, bass.ds(k, 1)], gu_w[:, bass.ds(k, 1)], ACT.Copy).then_inc(w_hi_ready, 1)
                nc.scalar.activation(dn_hi[:, bass.ds(k, 1)], dn_w[:, bass.ds(k, 1)], ACT.Copy).then_inc(w_hi_ready, 1)
            sc.wait_ge(ctx_low, 1)
            for b in range(BATCH):
                nc.scalar.activation(ctx_lo[:, :, b, :], ctxb[:], ACT.Copy,
                                     scale=c32[:, C_MINE + b:C_MINE + b + 1]).then_inc(ctx_lo_ready, 1)
            for g in range(GROUPS - 4, GROUPS):
                sc.wait_ge(diff_ready, 2 * (g + 1))
                sign_group(g % 2, slice(g * GROUP + 1, (g + 1) * GROUP + 1), slice(g * GROUP + 2, (g + 1) * GROUP + 2))
            for pr in range(BLOCK // 2):
                sc.wait_ge(masks_psum, 2 * (pr + 1))
                src = bank[4 + pr][:].bitcast(F16)[:, 0:2 * ROWS].rearrange("p (r j) -> p r j", r=2)
                nc.scalar.activation(up[:, 2 * pr:2 * pr + 2, :], src, ACT.Relu).then_inc(up_ready, 1)
            sc.wait_ge(up_ready, BLOCK // 2)
            nc.scalar.activation(upsum[:], up[:], ACT.Copy, scale=LABEL).then_inc(up_label_ready, 1)

            def roots(h):
                tiles = slice(h * BATCH, (h + 1) * BATCH)
                sc.wait_ge(var2_ready, h + 1)
                nc.scalar.activation(std[:, tiles], var[:, tiles], ACT.Sqrt).then_inc(std2_ready, 1)

            def high_tokens(h):
                sc.wait_ge(xT_psum, h + 1)
                nc.scalar.activation(xT_hi[:, h * 512:(h + 1) * 512], bank[6 + h][:], ACT.Copy).then_inc(xT_hi_ready, 1)

            def whole_tokens(h):
                sc.wait_ge(xT_lo_ready, h + 1)
                nc.scalar.activation(xT[:, h * 512:(h + 1) * 512], bank[6 + h][:], ACT.Copy).then_inc(xT_ready, 1)

            roots(0)
            high_tokens(0)
            roots(1)
            whole_tokens(0)
            high_tokens(1)
            whole_tokens(1)

            def silu_tile(v):
                sc.wait_ge(gu_psum, v + 1)
                if v >= 2:
                    sc.wait_ge(act_ready, v - 1)
                nc.scalar.activation(silu[:, v % 2, :], bank[v % 2][0:SUB, :], ACT.Silu).then_inc(silu_ready, 1)

            def high_part(v):
                sc.wait_ge(act_ready, v + 1)
                if v >= 2 * SUBS:
                    sc.wait_ge(down_psum, v - 2 * SUBS + 1)
                nc.scalar.activation(act_hi[:, v % (2 * SUBS), :], act[:, v % 2, :], ACT.Copy).then_inc(act_hi_ready, 1)

            for v in range(v_wide(UNITS - 1) + 2):
                if 1 <= v <= V_TOTAL:
                    high_part(v - 1)
                if v == V_SCORES + 1:
                    for h in range(HALVES):
                        sc.wait_ge(scoreT_psum, h + 1)
                        nc.scalar.activation(scoreT[:, h * 512:(h + 1) * 512], bank[6 + h][0:2 * EXPERTS, :], ACT.Copy)\
                            .then_inc(scoreT_ready, 1)
                for u in range(UNITS):
                    if v == v_wide(u) + 1:
                        sc.wait_ge(wide_psum, u + 1)
                        if u >= 2:
                            sc.wait_ge(scaled_ready, u - 1)
                        nc.scalar.activation(score_wide[:, u % 2], bank[6][:], ACT.Copy).then_inc(wide_ready, 1)
                if v < V_TOTAL:
                    silu_tile(v)
                if v == 1:
                    sc.wait_ge(actor_ones, 1)
                    for h in range(HALVES):
                        sc.wait_ge(actor_psum, h + 1)
                        sc.wait_ge(router_in, 80)
                        nc.scalar.activation(actor[0:ACTOR, h * 512:(h + 1) * 512], bank[4 + h][0:ACTOR, :], ACT.Gelu_apprx_tanh,
                                             bias=ba1[:, 0:1]).then_inc(actor_ready, 1)
                    sc.wait_ge(shifted_ready, 1)
                    nc.scalar.activation(prob[:], shifted[:], ACT.Exp).then_inc(exp_ready, 1)

        @block.vector
        def _(dve):
            steps = [0]

            def link(ins):
                steps[0] += 1
                ins.then_inc(dve_step, 1)
                dve.wait_ge(dve_step, steps[0])

            def moments(src, tiles, var_sem):
                for n in tiles:
                    nc.vector.bn_stats(stats[:, n, :], src[:, n, :]).then_inc(dve_step, 1)
                steps[0] += len(tiles)
                dve.wait_ge(dve_step, steps[0])
                for n in tiles:
                    nc.vector.bn_aggr(mv[:, n, :], stats[:, n, :]).then_inc(dve_step, 1)
                steps[0] += len(tiles)
                dve.wait_ge(dve_step, steps[0])
                own = slice(tiles[0], tiles[-1] + 1)
                nc.vector.tensor_scalar(var[:, own], mv[:, own, 1], 1e-5, None, ALU.add).then_inc(var_sem, 1)

            def normed(src, tiles, out_sem):
                own = slice(tiles[0], tiles[-1] + 1)
                link(nc.vector.reciprocal(rstd[:, own], std[:, own]))
                for n in tiles:
                    nc.vector.tensor_scalar(xn[:, n, :], src[:, n, :], mv[:, n, 0:1], rstd[:, n:n + 1],
                                            ALU.subtract, ALU.mult).then_inc(out_sem, 1)

            nc.vector.memset(ring[:], FAR).then_inc(ring_clear, 1)
            nc.vector.memset(DT[:], FAR).then_inc(ring_clear, 1)
            dve.wait_ge(x_in, 16)
            moments(x, range(TILES), var_ready)
            dve.wait_ge(std_ready, 1)
            normed(x, range(TILES), xn_ready)
            dve.wait_ge(ring_clear, 2)
            for n in range(TILES + 1):
                if n < TILES:
                    b = n % BATCH
                    dve.wait_ge(dot_psum, n // 2 * 2 + 2)
                    dve.wait_ge(ctxsum_ready, b // 2 + 1)
                    nc.vector.scalar_tensor_tensor(
                        out=DT[:, n, SKEW:SKEW + ROWS], in0=bank[2 + n // 2][:, (n % 2) * ROWS:(n % 2 + 1) * ROWS], scalar=-2.0,
                        in1=ctxsum[:, b * ROWS:(b + 1) * ROWS], op0=ALU.mult, op1=ALU.add).then_inc(crossed, 1)
                if n:
                    tile = DT[:, n - 1, SKEW:SKEW + ROWS]
                    dve.wait_ge(crossed, n)
                    dve.wait_ge(bb_ready, n)
                    nc.vector.tensor_scalar(tile, tile, bb[:, n - 1:n], 0.0, ALU.add, ALU.max).then_inc(sqdist_ready, 1)

            quarter = list(range(QUAD))
            mask = [QUAD - 1] + quarter[:-1]

            def sweep_step(u, base, group, head):
                before = (u - 1) % RING
                if u % GROUP == GROUP - 1 and (not head or u == RING - 1):
                    dve.wait_ge(diff_ready, group * 2 - 4)
                if head and u == 0:
                    dve.wait_ge(ring_clear, 2)
                    dve.wait_ge(c32_in, 16)
                else:
                    dve.wait_ge(sweep, base)
                nc.vector.tensor_tensor(out=mring[:, u, :], in0=ring[:, before, 0:LANE_COLS],
                                        in1=ring[:, before, 1:LANE_COLS + 1], op=ALU.min).then_inc(sweep, 1)
                nc.vector.stream_shuffle(out=ring[:, (u + 1) % RING, 0:1], in_=ring[:, before, LANE_COLS:LANE_COLS + 1],
                                         mask=mask).then_inc(sweep, 1)
                if u % GROUP == 0:
                    dve.wait_ge(dring_ready, group + 1)
                dve.wait_ge(sweep, base + 1)
                halo = c32[:, C_FIRST:C_FIRST + 1] if head and u == 0 else ring[:, u, 0:1]
                nc.vector.tensor_tensor_scan(out=ring[:, u, 1:LANE_COLS + 1], data0=mring[:, u, :],
                                             data1=Dring[:, u, :], initial=halo, op0=ALU.min, op1=ALU.add)\
                    .then_inc(sweep, 1)

            for u in range(RING):
                sweep_step(u, 3 * u, u // GROUP, True)
            with dve.Fori(1, TURNS) as k:
                for u in range(RING):
                    sweep_step(u, k * (3 * RING) + 3 * u, k * 4 + u // GROUP, False)

            dve.wait_ge(w_lo_ready, 2 * EXPERTS)
            link(nc.vector.memset(lab[:, :, 0:1], 0.0))
            link(nc.vector.memset(entry[:, BLOCKS - 1:BLOCKS], (2 * ROWS - 1) * LABEL))
            dve.wait_ge(c16_in, 16)
            link(nc.vector.tensor_copy(lab[:, 0, 1:ROWS + 1], half16(c16, H_LABEL)))

            def not_left(pr):
                dve.wait_ge(masks_psum, 2 * (pr + 1))
                src = bank[pr][:].bitcast(F16)[:, 0:2 * ROWS].rearrange("p (r j) -> p r j", r=2)
                nc.vector.tensor_scalar(notleft[:, 2 * pr:2 * pr + 2, :], src, 0.0, None, ALU.is_ge)\
                    .then_inc(notleft_ready, 1)

            not_left(0)
            for r in range(BLOCK):
                src, dst = lab[:, r % 2], lab[:, (r + 1) % 2]
                dve.wait_ge(up_ready, r // 2 + 1)
                nc.vector.tensor_tensor(out=lab_t[:], in0=src[:, 1:ROWS + 1], in1=up[:, r, :], op=ALU.min)\
                  .then_inc(dve_step, 1)
                if r % 2 and r < BLOCK - 1:
                    not_left(r // 2 + 1)
                steps[0] += 1
                dve.wait_ge(dve_step, steps[0])
                link(nc.vector.tensor_tensor(out=lab_e[:], in0=lab_t[:], in1=src[:, 0:ROWS], op=ALU.max))
                dve.wait_ge(notleft_ready, r // 2 + 1)
                scan = nc.vector.tensor_tensor_scan(out=dst[:, 1:ROWS + 1], data0=notleft[:, r, :], data1=lab_e[:],
                                                    initial=0.0, op0=ALU.max, op1=ALU.min)
                if r < BLOCK - 1:
                    link(scan)
                else:
                    scan.then_inc(labels_ready, 1)
            for k in range(BLOCKS - 1, 0, -1):
                if k >= DMA_BLOCKS:
                    i = BLOCKS - 1 - k
                    dve.wait_ge(map_psum, i // 2 * 2 + 2)
                    block_labels = bank[i // 2][0:BATCH, (i % 2) * ROWS:(i % 2 + 1) * ROWS]
                else:
                    block_labels = block_map[:, k, :]
                if k == DMA_BLOCKS - 1:
                    dve.wait_ge(map_moved, 16 * BATCH)
                if k < BLOCKS - 1:
                    dve.wait_ge(entries_ready, BLOCKS - 1 - k)
                nc.vector.scalar_tensor_tensor(out=junk[0:BATCH, :], in0=c16[0:BATCH, H_LABEL:H_LABEL + ROWS],
                                               scalar=entry[:, k:k + 1], in1=block_labels,
                                               op0=ALU.is_equal, op1=ALU.mult,
                                               accum_out=entry[:, k - 1:k]).then_inc(entries_ready, 1)
            dve.wait_ge(entry_psum, 1)
            link(nc.vector.scalar_tensor_tensor(out=junk32[:], in0=bank[6][:, 0:BLOCKS], scalar=1.0,
                                                in1=c32[:, C_DIAG:C_DIAG + BLOCKS], op0=ALU.mult, op1=ALU.mult,
                                                accum_out=entry0[:]))
            dve.wait_ge(exit_ready, 1)
            def path_row(r):
                nc.vector.scalar_tensor_tensor(out=path[:, r, :], in0=half16(c16, H_TWICE4), scalar=q[:, r:r + 1],
                                               in1=within[:, r, :], op0=ALU.is_gt, op1=ALU.mult).then_inc(path_ready, 1)

            for r in range(BLOCK - 1, -1, -1):
                table, bound = (H_TWICE2, q[:, r + 1:r + 2]) if r < BLOCK - 1 else (H_TWICE, entry0[:, 0:1])
                nc.vector.tensor_scalar(within[:, r, :], half16(c16, table), bound, None, ALU.is_lt).then_inc(dve_step, 1)
                steps[0] += 1
                if r < BLOCK - 1:
                    path_row(r + 1)
                dve.wait_ge(dve_step, steps[0])
                link(nc.vector.tensor_tensor_reduce(out=junk[:], in0=within[:, r, :], in1=exit2[:, r, :], scale=1.0,
                                                    scalar=0.0, op0=ALU.mult, op1=ALU.max, accum_out=q[:, r:r + 1]))
            path_row(0)
            dve.wait_ge(gate_ready, 1)

            def residual(h):
                tiles = slice(h * BATCH, (h + 1) * BATCH)
                dve.wait_ge(attn_psum, h + 1)
                nc.vector.scalar_tensor_tensor(out=x1[:, tiles, :], in0=bank[h][:].rearrange("p (b d) -> p b d", b=BATCH),
                                               scalar=tg[:, 0:1], in1=x[:, tiles, :], op0=ALU.mult, op1=ALU.add)\
                    .then_inc(x1_ready, 1)

            def low_tokens(h):
                dve.wait_ge(xT_hi_ready, h + 1)
                nc.vector.tensor_tensor(out=xT_lo[:, h * 512:(h + 1) * 512], in0=bank[6 + h][:],
                                        in1=xT_hi[:, h * 512:(h + 1) * 512].bitcast(F32), op=ALU.subtract)\
                    .then_inc(xT_lo_ready, 1)

            tiles0, tiles1 = range(BATCH), range(BATCH, TILES)
            residual(0)
            dve.wait_ge(x1_ready, 1)
            moments(x1, tiles0, var2_ready)
            residual(1)
            dve.wait_ge(std2_ready, 1)
            normed(x1, tiles0, xn2_ready)
            dve.wait_ge(x1_ready, 2)
            moments(x1, tiles1, var2_ready)
            low_tokens(0)
            dve.wait_ge(std2_ready, 2)
            normed(x1, tiles1, xn2_ready)
            low_tokens(1)

            def wide(a, n):
                return a.unsqueeze(2).to_broadcast([P, TILES, n])

            top, total_prob, inv, best, where, spare = tile1

            def ranks():
                dve.wait_ge(router_psum, 1)
                link(nc.vector.tensor_copy(logit[:], bank[6][:, 0:64].rearrange("p (n e) -> p n e", n=TILES)))
                link(nc.vector.tensor_reduce(out=top[:], in_=logit[:], axis=AX.X, op=ALU.max))
                nc.vector.tensor_tensor(out=shifted[:], in0=logit[:], in1=wide(top[:], EXPERTS), op=ALU.subtract)\
                    .then_inc(shifted_ready, 1)
                mine = logit[:].unsqueeze(3).to_broadcast([P, TILES, EXPERTS, EXPERTS])
                others = logit[:].unsqueeze(2).to_broadcast([P, TILES, EXPERTS, EXPERTS])
                earlier = c32[:, C_EARLIER:C_EARLIER + 64].rearrange("p (e o) -> p e o", e=EXPERTS)
                link(nc.vector.tensor_tensor(out=pair[:], in0=others, in1=mine, op=ALU.is_equal))
                link(nc.vector.tensor_tensor(out=pair[:], in0=pair[:],
                                             in1=earlier.unsqueeze(1).to_broadcast([P, TILES, EXPERTS, EXPERTS]),
                                             op=ALU.mult))
                link(nc.vector.tensor_tensor(out=pair2[:], in0=others, in1=mine, op=ALU.is_gt))
                link(nc.vector.tensor_tensor(out=pair[:], in0=pair[:], in1=pair2[:], op=ALU.add))
                link(nc.vector.tensor_reduce(out=rank[:], in_=pair[:], axis=AX.X, op=ALU.add))

            def counts():
                dve.wait_ge(choice_psum, 1)
                link(nc.vector.tensor_scalar(choice[:], bank[7][:, 0:64].rearrange("p (n e) -> p n e", n=TILES)[:, :, 0:MAX_K],
                                             -30.0, 30.0, ALU.max, ALU.min))
                link(nc.vector.tensor_reduce(out=best[:], in_=choice[:], axis=AX.X, op=ALU.max))
                link(nc.vector.tensor_tensor(out=first[:], in0=choice[:], in1=wide(best[:], MAX_K), op=ALU.is_equal))
                order = c32[:, C_ORDER:C_ORDER + MAX_K].unsqueeze(1).to_broadcast([P, TILES, MAX_K])
                link(nc.vector.tensor_tensor(out=first[:], in0=first[:], in1=order, op=ALU.mult))
                link(nc.vector.tensor_reduce(out=where[:], in_=first[:], axis=AX.X, op=ALU.max))
                link(nc.vector.tensor_tensor(out=rank[:], in0=rank[:], in1=wide(where[:], EXPERTS), op=ALU.add))
                link(nc.vector.tensor_scalar(rank[:], rank[:], MAX_K + 1.0, tg[:, 1:2], ALU.is_lt, ALU.mult))

            def scores():
                dve.wait_ge(exp_ready, 1)
                link(nc.vector.tensor_reduce(out=total_prob[:], in_=prob[:], axis=AX.X, op=ALU.add))
                link(nc.vector.reciprocal(inv[:], total_prob[:]))
                link(nc.vector.tensor_tensor(out=prob[:], in0=prob[:], in1=wide(inv[:], EXPERTS), op=ALU.mult))
                link(nc.vector.tensor_tensor(out=prob[:], in0=prob[:], in1=rank[:], op=ALU.mult))
                link(nc.vector.tensor_copy(score_r[:], prob[:]))
                link(nc.vector.tensor_copy(score2[:, :, 0:EXPERTS], score_r[:].bitcast(F32)))
                nc.vector.tensor_tensor(out=score2[:, :, EXPERTS:2 * EXPERTS], in0=prob[:], in1=score_r[:].bitcast(F32),
                                        op=ALU.subtract).then_inc(score_ready, 1)

            def product(v):
                dve.wait_ge(silu_ready, v + 1)
                if v >= 2:
                    dve.wait_ge(act_hi_ready, v - 1)
                    dve.wait_ge(act_lo_ready, v - 1)
                nc.vector.tensor_tensor(out=act[:, v % 2, :], in0=silu[:, v % 2, :], in1=bank[2 + v % 2][0:SUB, :],
                                        op=ALU.mult).then_inc(act_ready, 1)

            def low_part(v):
                dve.wait_ge(act_ready, v + 1)
                dve.wait_ge(act_hi_ready, v + 1)
                if v >= 2 * SUBS:
                    dve.wait_ge(down_psum, v - 2 * SUBS + 1)
                slot = v % (2 * SUBS)
                nc.vector.tensor_tensor(out=act_lo[:, slot, :], in0=act[:, v % 2, :],
                                        in1=act_hi[:, slot, :].bitcast(F32), op=ALU.subtract).then_inc(act_lo_ready, 1)

            def scale(u):
                h, e = units[u]
                dve.wait_ge(down_psum, SUBS * (u + 1))
                dve.wait_ge(wide_ready, u + 1)
                if u >= 2 and adds(u - 2):
                    dve.wait_ge(acc_ready, adds(u - 2))
                if u - 2 == EXPERTS - 1:
                    dve.wait_ge(last_psum, 1)
                dst = scaled[:, u % 2] if e else acc[:, h]
                nc.vector.tensor_tensor(out=dst, in0=bank[4 + u % 2][:], in1=score_wide[:, u % 2], op=ALU.mult)\
                    .then_inc(scaled_ready, 1)

            def finish(h, last):
                tiles = slice(h * BATCH, (h + 1) * BATCH)
                if last:
                    dve.wait_ge(last_psum, h + 1)
                    dve.wait_ge(partial_ready, h + 1)
                else:
                    dve.wait_ge(acc_psum, h + 1)
                nc.vector.tensor_tensor(out=result[:, tiles, :], in0=bank[7][:].rearrange("p (b d) -> p b d", b=BATCH),
                                        in1=(result if last else x1)[:, tiles, :], op=ALU.add)\
                    .then_inc(result_ready if last else partial_ready, 1)

            for v in range(v_turn(HALVES - 1) + 1):
                if v < V_TOTAL:
                    product(v)
                if 1 <= v <= V_TOTAL:
                    low_part(v - 1)
                if v == 1:
                    ranks()
                if v == 2:
                    counts()
                if v == 3:
                    scores()
                for h in range(HALVES):
                    if v == v_part(h) + 1:
                        finish(h, False)
                    if v == v_turn(h) + 1:
                        finish(h, True)
                for u in range(UNITS):
                    if v == v_scale(u):
                        scale(u)
            finish(HALVES - 1, True)

        @block.tensor
        def _(pe):
            mm = nc.tensor.matmul

            def warm_up(count, at=0):
                for _ in range(count):
                    last = mm(bank[at][:], warm_w[:], warm_in[:], start=True, stop=True)
                last.then_inc(warm, 1)

            pe.wait_ge(warm_clear, 2)
            warm_up(14)
            pe.wait_ge(cleared, 1)
            pe.wait_ge(c32_in, 16)
            for n in range(BATCH):
                pe.wait_ge(xn_ready, n + 1)
                nc.tensor.transpose(bank[0][:, n * P:(n + 1) * P], xn[:, n, :], ident).then_inc(xnT_psum, 1)
            pe.wait_ge(ctxsq_ready, 1)
            for h in range(2):
                mm(bank[6 + h][:], ones[:], ctxsq[:, h * 512:(h + 1) * 512], start=True, stop=True).then_inc(ctxsum_psum, 1)

            def dots(h):
                pe.wait_ge(xnT_ready, h + 1)
                for b in range(BATCH):
                    n = h * BATCH + b
                    mm(bank[2 + n // 2][:, (n % 2) * ROWS:(n % 2 + 1) * ROWS], xnT[:, n * P:(n + 1) * P],
                       ctxT[:, b * ROWS:(b + 1) * ROWS], start=True, stop=True).then_inc(dot_psum, 1)

            for n in range(BATCH, TILES):
                pe.wait_ge(xn_ready, n + 1)
                nc.tensor.transpose(bank[1][:, (n - BATCH) * P:(n - BATCH + 1) * P], xn[:, n, :], ident).then_inc(xnT_psum, 1)
            for h in range(HALVES):
                dots(h)
            pe.wait_ge(gates_in, 16)
            mm(bank[1][:, 0:2], ones[0:1, :], gin[:], start=True, stop=True).then_inc(gate_psum, 1)
            pe.wait_ge(warm, 1)
            pe.wait_ge(signs_ready, 2 * GROUPS)
            warm_up(16)
            pe.wait_ge(c16_in, 16)
            pe.wait_ge(masks_moved, 16 * 2 * HALVES * CHUNKS)
            pe.wait_ge(sqdist_ready, TILES)
            pe.wait_ge(xnT_ready, 2)
            for r in range(BLOCK):
                for plane in range(2):
                    for h in range(HALVES):
                        at = (r % 2) * ROWS + h * P
                        src = KT[:, h, plane].rearrange("p b (k r) -> p (b k) r", r=BLOCK)[:, :, r]
                        last = nc.tensor.transpose(bank[plane * 4 + r // 2][:].bitcast(F16)[:, at:at + P], src, ident16)
                last.then_inc(masks_psum, 1)
            pe.wait_ge(labels_ready, 1)
            pe.wait_ge(up_ready, BLOCK // 2)
            for k in range(BLOCKS - 1, DMA_BLOCKS - 1, -1):
                i = BLOCKS - 1 - k
                mm(bank[i // 2][0:BATCH, (i % 2) * ROWS:(i % 2 + 1) * ROWS], ident16[:, k::BLOCKS], lab[:, 0, 1:ROWS + 1],
                   start=True, stop=True).then_inc(map_psum, 1)
            pe.wait_ge(entries_ready, BLOCKS - 9)
            warm_up(8, 7)
            pe.wait_ge(entries_ready, BLOCKS - 1)
            pe.wait_ge(gate_ready, 1)
            mm(bank[6][:, 0:BLOCKS], c32[0:BATCH, C_BATCH:C_BATCH + P], entry[:], start=True, stop=True)\
                .then_inc(entry_psum, 1)
            warm_up(9, 7)
            pe.wait_ge(ctx_hi_ready, 1 + BATCH)
            pe.wait_ge(ctx_lo_ready, BATCH)
            pe.wait_ge(up_ready, BLOCK // 2)
            pe.wait_ge(notleft_ready, BLOCK // 2)
            for i, r in enumerate(range(BLOCK - 1, -1, -1)):
                pe.wait_ge(path_ready, i + 1)
                for h in range(HALVES):
                    tok = path[:, r, h * P:(h + 1) * P]
                    mm(bank[h][:], tok, ctx_hi[:, r], start=(i == 0), stop=False)
                    last = mm(bank[h][:], tok, ctx_lo[:, r], start=False, stop=(i == BLOCK - 1))
                    if i == BLOCK - 1:
                        last.then_inc(attn_psum, 1)
            warm_up(8, 7)
            for n in range(TILES):
                pe.wait_ge(xn2_ready, n + 1)
                last = nc.tensor.transpose(bank[6 + n // 4][:, (n % 4) * P:(n % 4 + 1) * P], xn[:, n, :], ident)
                if n % 4 == 3:
                    last.then_inc(xT_psum, 1)

            def split_mm(dst, w_hi, w_lo, a_hi, a_lo, start, stop):
                mm(dst, w_hi, a_hi, start=start, stop=False)
                mm(dst, w_hi, a_lo, start=False, stop=False)
                return mm(dst, w_lo, a_hi, start=False, stop=stop)

            def gate_up(v):
                h, e = units[v // SUBS]
                m = v % SUBS
                if v % (SUBS * EXPERTS) == 0:
                    pe.wait_ge(xT_lo_ready, h + 1)
                    pe.wait_ge(xT_hi_ready, h + 1)
                tok = slice(h * 512, (h + 1) * 512)
                for part in range(2):
                    if v >= 2:
                        pe.wait_ge(act_ready if part else silu_ready, v - 1)
                    col = slice(m * SUB, (m + 1) * SUB)
                    last = split_mm(bank[2 * part + v % 2][0:SUB, :], gu_hi[:, e, part, col], gu_lo[:, e, part, col],
                                    xT_hi[:, tok], xT_lo[:, tok], True, True)
                last.then_inc(gu_psum, 1)

            def down(v):
                u, m = v // SUBS, v % SUBS
                h, e = units[u]
                pe.wait_ge(act_hi_ready, v + 1)
                pe.wait_ge(act_lo_ready, v + 1)
                if m == 0 and u >= 2:
                    pe.wait_ge(scaled_ready, u - 1)
                slot, col = v % (2 * SUBS), slice(m * DIM, (m + 1) * DIM)
                split_mm(bank[4 + u % 2][:], dn_hi[:, e, col], dn_lo[:, e, col], act_hi[:, slot, :], act_lo[:, slot, :],
                         m == 0, m == SUBS - 1).then_inc(down_psum, 1)

            def router_actor():
                pe.wait_ge(router_in, 80)
                pe.wait_ge(xT_ready, HALVES)
                pe.wait_ge(xT_hi_ready, HALVES)
                for h in range(HALVES):
                    mm(bank[4 + h][0:ACTOR, :], wa1[:], xT[:, h * 512:(h + 1) * 512], start=True, stop=True)\
                        .then_inc(actor_psum, 1)
                for n in range(TILES):
                    last = mm(bank[6][:, n * EXPERTS:(n + 1) * EXPERTS], xT[:, n * P:(n + 1) * P], wr[:],
                              start=True, stop=True)
                last.then_inc(router_psum, 1)
                pe.wait_ge(actor_ready, HALVES)
                for n in range(TILES):
                    dst = bank[7][:, n * EXPERTS:n * EXPERTS + MAX_K]
                    last = mm(dst, actor[0:ACTOR + 1, n * P:(n + 1) * P], wa2[:], start=True, stop=True)
                last.then_inc(choice_psum, 1)

            pe.wait_ge(w_lo_ready, 2 * EXPERTS)
            for v in range(v_turn(HALVES - 1) + 1):
                if v < V_TOTAL:
                    gate_up(v)
                if DOWN_LAG <= v < V_TOTAL + DOWN_LAG:
                    down(v - DOWN_LAG)
                if v == 1:
                    router_actor()
                if v == V_SCORES:
                    pe.wait_ge(score_ready, 1)
                    for h in range(HALVES):
                        for b in range(BATCH):
                            last = nc.tensor.transpose(bank[6 + h][0:2 * EXPERTS, b * P:(b + 1) * P],
                                                       score2[:, h * BATCH + b, :], ident)
                        last.then_inc(scoreT_psum, 1)
                for u in range(UNITS):
                    if v == v_wide(u):
                        if u:
                            pe.wait_ge(wide_ready, u)
                        else:
                            pe.wait_ge(scoreT_ready, HALVES)
                            pe.wait_ge(pick_ready, 1)
                        h, e = units[u]
                        mm(bank[6][:], pick[:, e, :], scoreT[:, h * 512:(h + 1) * 512], start=True, stop=True)\
                            .then_inc(wide_psum, 1)
                for h in range(HALVES):
                    if v == v_part(h):
                        pe.wait_ge(acc_ready, adds((h + 1) * EXPERTS - 1))
                        if h:
                            pe.wait_ge(result_ready, h)
                        for b in range(BATCH):
                            last = nc.tensor.transpose(bank[7][:, b * P:(b + 1) * P], acc[:, h, b * P:(b + 1) * P], ident)
                        last.then_inc(acc_psum, 1)
                    if v == v_turn(h):
                        u = (h + 1) * EXPERTS - 1
                        pe.wait_ge(scaled_ready, u + 1)
                        pe.wait_ge(partial_ready, h + 1)
                        for b in range(BATCH):
                            last = nc.tensor.transpose(bank[7][:, b * P:(b + 1) * P], scaled[:, u % 2, b * P:(b + 1) * P], ident)
                        last.then_inc(last_psum, 1)


def constants():
    import numpy as np

    c32 = np.zeros((P, C_WIDTH), np.float32)
    p = np.arange(P)
    c32[p, C_IDENT + p] = 1
    c32[p, C_DIAG + p % BLOCKS] = 1
    c32[p // BLOCKS, C_BATCH + p] = 1
    e = np.arange(EXPERTS)
    c32[:, C_EARLIER:C_EARLIER + 64] = (e[None, :] < e[:, None]).reshape(-1)
    c32[:, C_ORDER:C_ORDER + MAX_K] = MAX_K - np.arange(MAX_K)
    c32[p, C_MINE + p // QUAD] = 1
    c32[p, C_PICK + p % EXPERTS] = 1
    c32[:, C_FIRST] = np.where(p % QUAD == 0, 0.0, FAR)
    c16 = np.zeros((P, H_WIDTH), np.float16)
    c16[p, H_IDENT + p] = 1
    j = np.arange(ROWS)
    for at, v in ((H_LABEL, 2 * j + 1), (H_TWICE, 2 * j), (H_TWICE2, 2 * j + 2), (H_TWICE4, 2 * j + 4)):
        c16[:, at:at + ROWS] = v * LABEL
    return c32, c16


def kernel(x, ctx_1024, g_xattn, g_ffn, L0_ffn_router_w, L0_ffn_actor_w1, L0_ffn_actor_b1, L0_ffn_actor_w2,
           L0_ffn_actor_b2, L0_ffn_gate_w, L0_ffn_up_w, L0_ffn_down_w):
    import numpy as np
    import concourse.bacc as bacc
    from concourse.bass_utils import run_bass_kernel_spmd

    a = np.asarray
    c32, c16 = constants()
    arrays = {
        "x_tok": a(x).reshape(BATCH, HALVES, P, DIM).transpose(2, 1, 0, 3).reshape(P, TILES, DIM),
        "ctx_t": a(ctx_1024).reshape(BATCH * ROWS, DIM).T,
        "ctx_blk": a(ctx_1024).reshape(BATCH * BLOCKS, BLOCK, DIM),
        "gates": np.concatenate([a(g_xattn), a(g_ffn)]).reshape(1, 2),
        "w_gate": a(L0_ffn_gate_w).transpose(2, 0, 1),
        "w_up": a(L0_ffn_up_w).transpose(2, 0, 1),
        "w_down": a(L0_ffn_down_w).reshape(EXPERTS, DIM, SUBS, SUB).transpose(3, 0, 2, 1).reshape(SUB, EXPERTS, SUBS * DIM),
        "w_router": a(L0_ffn_router_w).T,
        "w_a1": a(L0_ffn_actor_w1).T,
        "b_a1": a(L0_ffn_actor_b1).reshape(ACTOR, 1),
        "w_a2": a(L0_ffn_actor_w2).T,
        "b_a2": a(L0_ffn_actor_b2).reshape(1, MAX_K),
        "const32": c32,
        "const16": c16,
    }
    arrays = {k: np.ascontiguousarray(v) for k, v in arrays.items()}
    nc = bacc.Bacc("TRN2", target_bir_lowering=False, num_devices=1)
    aps = [nc.dram_tensor(k, v.shape, mybir.dt.from_np(v.dtype), kind="ExternalInput").ap() for k, v in arrays.items()]
    out = nc.dram_tensor("out", (P, HALVES, BATCH, DIM), mybir.dt.float32, kind="ExternalOutput").ap()
    dist_dram = nc.dram_tensor("dist_dram", (BATCH * ROWS, D_WIDTH), mybir.dt.float32, kind="Internal").ap()
    mask_dram = nc.dram_tensor("mask_dram", (BATCH, ROWS, 2, M_WIDTH), mybir.dt.float16, kind="Internal").ap()
    build(nc, *aps, dist_dram, mask_dram, out)
    r = run_bass_kernel_spmd(nc, [arrays], core_ids=[0])
    got = a(r.results[0]["out"])
    return got.transpose(2, 1, 0, 3).reshape(BATCH, ROWS, DIM)
```
